# Optimizing a Trainium2 kernel written in Bass

```python
import numpy as np
import jax
import jax.numpy as jnp

def _softmax(x, axis=-1):
    return jax.nn.softmax(x, axis=axis)

def _gelu(x):
    return jax.nn.gelu(x, approximate=True)

def _silu(x):
    return jax.nn.silu(x)

def _sigmoid(x):
    return jax.nn.sigmoid(x)

def _layernorm(x, axis=-1, eps=1e-05):
    m = jnp.mean(x, axis=axis, keepdims=True)
    v = jnp.var(x, axis=axis, keepdims=True)
    return (x - m) / jnp.sqrt(v + eps)

def _scatter_add(tgt, idx, src, axis=0):
    return tgt.at[idx].add(src)

def _segment_sum(src, seg, n):
    return jax.ops.segment_sum(src, seg, n)
kernel_name = 'mk_prb_d1_jaxref_r8_3d47c7'

def setup_inputs(seed: int=0):
    np.random.seed(seed)
    _w = jnp.asarray

    def _L0_attn_setup():
        import jax, jax.numpy as jnp
        import numpy as np
        B, N, D, H = (4, 512, 128, 16)
        HD = D // H
        EPS_NORM = 1e-12
        EPS_LN = 1e-05

        def _silu(x):
            return x * jax.nn.sigmoid(x)

        def _simple_gla(q, k, v, f):
            qT = jnp.moveaxis(q, 1, 0)
            kT = jnp.moveaxis(k, 1, 0)
            vT = jnp.moveaxis(v, 1, 0)
            fT = jnp.moveaxis(f, 1, 0)

            def step(S, inp):
                qt, kt, vt, ft = inp
                S = jnp.exp(ft)[..., None, None] * S + kt[..., :, None] * vt[..., None, :]
                o = jnp.einsum('bhk,bhkv->bhv', qt, S)
                return (S, o)
            S0 = jnp.zeros((q.shape[0], q.shape[2], q.shape[3], v.shape[3]), q.dtype)
            _, o = jax.lax.scan(step, S0, (qT, kT, vT, fT))
            return jnp.moveaxis(o, 0, 1)
        key = jax.random.key(seed)
        ks = jax.random.split(key, 9)
        s = 0.02
        return {'x': jax.random.normal(ks[0], (B, N, D), jnp.float32), 'Wq': jax.random.normal(ks[1], (D, D), jnp.float32) * s, 'Wk': jax.random.normal(ks[2], (D, D), jnp.float32) * s, 'Wv': jax.random.normal(ks[3], (D, D), jnp.float32) * s, 'Wf': jax.random.normal(ks[4], (H, D), jnp.float32) * s, 'Wg1': jax.random.normal(ks[5], (HD, D), jnp.float32) * s, 'Wg2': jax.random.normal(ks[6], (D, HD), jnp.float32) * s, 'ln_w': jnp.ones((D,), jnp.float32), 'Wo': jax.random.normal(ks[7], (D, D), jnp.float32) * s}
    _L0_attn_in = _L0_attn_setup()

    def _L0_ffn_setup():
        import jax, jax.numpy as jnp
        import numpy as np
        NUM_EXPERTS = 8
        TOP_K = 2
        D_MODEL = 128
        D_HID = 512
        BATCH, SEQ = (2, 256)
        key = jax.random.key(seed)
        ks = jax.random.split(key, 5)
        s = 0.02
        return {'x': jax.random.normal(ks[0], (BATCH, SEQ, D_MODEL), dtype=jnp.float32), 'Wg': jax.random.normal(ks[1], (D_MODEL, NUM_EXPERTS), dtype=jnp.float32) * s, 'bg': jnp.zeros((NUM_EXPERTS,), dtype=jnp.float32), 'W0': jax.random.normal(ks[2], (NUM_EXPERTS, D_MODEL, D_HID), dtype=jnp.float32) * s, 'b0': jnp.zeros((NUM_EXPERTS, D_HID), dtype=jnp.float32), 'W1': jax.random.normal(ks[3], (NUM_EXPERTS, D_MODEL, D_HID), dtype=jnp.float32) * s, 'b1': jnp.zeros((NUM_EXPERTS, D_HID), dtype=jnp.float32), 'W2': jax.random.normal(ks[4], (NUM_EXPERTS, D_HID, D_MODEL), dtype=jnp.float32) * s, 'b2': jnp.zeros((NUM_EXPERTS, D_MODEL), dtype=jnp.float32)}
    _L0_ffn_in = _L0_ffn_setup()
    _d = {'L0_attn_x': _L0_attn_in['x'], 'L0_attn_Wq': _L0_attn_in['Wq'], 'L0_attn_Wk': _L0_attn_in['Wk'], 'L0_attn_Wv': _L0_attn_in['Wv'], 'L0_attn_Wf': _L0_attn_in['Wf'], 'L0_attn_Wg1': _L0_attn_in['Wg1'], 'L0_attn_Wg2': _L0_attn_in['Wg2'], 'L0_attn_ln_w': _L0_attn_in['ln_w'], 'L0_attn_Wo': _L0_attn_in['Wo'], 'L0_ffn_Wg': _L0_ffn_in['Wg'], 'L0_ffn_bg': _L0_ffn_in['bg'], 'L0_ffn_W0': _L0_ffn_in['W0'], 'L0_ffn_b0': _L0_ffn_in['b0'], 'L0_ffn_W1': _L0_ffn_in['W1'], 'L0_ffn_b1': _L0_ffn_in['b1'], 'L0_ffn_W2': _L0_ffn_in['W2'], 'L0_ffn_b2': _L0_ffn_in['b2']}
    _x0 = _d['L0_attn_x']
    _d['L0_attn_x'] = jax.random.normal(jax.random.fold_in(jax.random.key(seed), 1), (32, 256, 128), dtype=_x0.dtype)
    del _x0
    return _d

def reference(L0_attn_x, L0_attn_Wq, L0_attn_Wk, L0_attn_Wv, L0_attn_Wf, L0_attn_Wg1, L0_attn_Wg2, L0_attn_ln_w, L0_attn_Wo, L0_ffn_Wg, L0_ffn_bg, L0_ffn_W0, L0_ffn_b0, L0_ffn_W1, L0_ffn_b1, L0_ffn_W2, L0_ffn_b2):

    def _L0_attn_ref(x, Wq, Wk, Wv, Wf, Wg1, Wg2, ln_w, Wo):
        import jax, jax.numpy as jnp
        import numpy as np
        B, N, D, H = (4, 512, 128, 16)
        HD = D // H
        EPS_NORM = 1e-12
        EPS_LN = 1e-05

        def _silu(x):
            return x * jax.nn.sigmoid(x)

        def _simple_gla(q, k, v, f):
            qT = jnp.moveaxis(q, 1, 0)
            kT = jnp.moveaxis(k, 1, 0)
            vT = jnp.moveaxis(v, 1, 0)
            fT = jnp.moveaxis(f, 1, 0)

            def step(S, inp):
                qt, kt, vt, ft = inp
                S = jnp.exp(ft)[..., None, None] * S + kt[..., :, None] * vt[..., None, :]
                o = jnp.einsum('bhk,bhkv->bhv', qt, S)
                return (S, o)
            S0 = jnp.zeros((q.shape[0], q.shape[2], q.shape[3], v.shape[3]), q.dtype)
            _, o = jax.lax.scan(step, S0, (qT, kT, vT, fT))
            return jnp.moveaxis(o, 0, 1)
        b, n, d = x.shape
        q = _silu(x @ Wq.T).reshape(b, n, H, HD)
        k = _silu(x @ Wk.T).reshape(b, n, H, HD)
        v = _silu(x @ Wv.T).reshape(b, n, H, HD)
        f = jax.nn.log_sigmoid(x @ Wf.T)
        k = k / jnp.maximum(jnp.linalg.norm(k, axis=-1, keepdims=True), EPS_NORM)
        o = _simple_gla(q, k, v, f).reshape(b, n, d)
        gate = jax.nn.sigmoid(x @ Wg1.T @ Wg2.T)
        o = o * gate
        mu = jnp.mean(o, axis=-1, keepdims=True)
        xc = o - mu
        var = jnp.mean(xc * xc, axis=-1, keepdims=True)
        o = xc / jnp.sqrt(var + EPS_LN) * ln_w
        return o @ Wo.T

    def _L0_ffn_ref(x, Wg, bg, W0, b0, W1, b1, W2, b2):
        import jax, jax.numpy as jnp
        import numpy as np
        NUM_EXPERTS = 8
        TOP_K = 2
        D_MODEL = 128
        D_HID = 512
        BATCH, SEQ = (2, 256)
        n, s, d = x.shape
        gate_logits = x @ Wg + bg
        top_vals, top_idx = jax.lax.top_k(gate_logits, TOP_K)
        w = jax.nn.softmax(top_vals, axis=-1)
        combine = jnp.sum(jax.nn.one_hot(top_idx, NUM_EXPERTS, dtype=x.dtype) * w[..., None], axis=-2)
        xf = x.reshape(n * s, d)
        h = jnp.einsum('td,edh->eth', xf, W0) + b0[:, None, :]
        g = jax.nn.silu(jnp.einsum('td,edh->eth', xf, W1) + b1[:, None, :])
        y = jnp.einsum('eth,ehd->etd', h * g, W2) + b2[:, None, :]
        out = jnp.einsum('te,etd->td', combine.reshape(n * s, NUM_EXPERTS), y)
        return out.reshape(n, s, d)
    x = L0_attn_x
    xn = _layernorm(x, axis=-1)
    x = x + _L0_attn_ref(xn, L0_attn_Wq, L0_attn_Wk, L0_attn_Wv, L0_attn_Wf, L0_attn_Wg1, L0_attn_Wg2, L0_attn_ln_w, L0_attn_Wo) + _L0_ffn_ref(xn, L0_ffn_Wg, L0_ffn_bg, L0_ffn_W0, L0_ffn_b0, L0_ffn_W1, L0_ffn_b1, L0_ffn_W2, L0_ffn_b2)
    return x

_drawn_inputs = setup_inputs


def setup_inputs(seed=0):
    import zlib

    import numpy as np

    out = dict(_drawn_inputs(seed))
    spreads = {'L0_attn_ln_w': (1.0, 0.6),
     'L0_ffn_bg': (0.0, 0.1),
     'L0_ffn_b0': (0.0, 0.8),
     'L0_ffn_b1': (0.0, 0.8),
     'L0_ffn_b2': (0.0, 0.392)}
    factors = {'L0_attn_Wf': 15.751,
     'L0_attn_Wg1': 8.0,
     'L0_attn_Wg2': 8.0,
     'L0_ffn_W0': 6.291,
     'L0_ffn_W1': 6.349,
     'L0_ffn_W2': 5.745}
    for name, (base, spread) in spreads.items():
        noise = np.random.default_rng([zlib.crc32(name.encode()), seed]).standard_normal(out[name].shape)
        drawn = base * np.exp(spread * noise) if base else spread * noise
        out[name] = jnp.asarray(drawn.astype(out[name].dtype))
    for name, factor in factors.items():
        out[name] = (out[name] * factor).astype(out[name].dtype)
    return out
```

```python
from contextlib import ExitStack

import numpy as np

import concourse.bass as bass
from concourse import mybir

F32 = mybir.dt.float32
F32R = mybir.dt.float32r
BF16 = mybir.dt.bfloat16
I32 = mybir.dt.int32
U32 = mybir.dt.uint32
ALU = mybir.AluOpType
ACT = mybir.ActivationFunctionType
AX = mybir.AxisListType

P = 128
D = 128
H = 16
HD = D // H
SEQ = 256
T = 32 * SEQ
TILES = T // P
UNIT = 512
UNITS = T // UNIT
UT = UNIT // P
E = 8
HID = 512
HC = HID // P
BLOCK = 512
HALF = BLOCK // 2
SUBS = HALF // P
MAX_BLOCKS = 2 * T // BLOCK + E - 1
MIN_BLOCKS = 2 * T // BLOCK
TABLE = (MAX_BLOCKS + 1) * BLOCK // P
EPS = 1e-5
NORM_MIN_SQ = 1e-24
FOLD = 18
POOL_V = (0, 2, 4, 6)
DVE_V = tuple(v for v in range(HD) if v not in POOL_V)
Q, K, V, F, L, G = range(6)


def build(nc, x, w_proj, wg1, wg2t, wot, ln_w, gate_b, w0, w1, w2, b0, b1, b2,
          ident_in, below_in, heads_in, spread_in, collect_in, center_in, iota_in, token_in, rank_in, out):
    xn_dram = nc.dram_tensor("xn_dram", [T, D], F32, kind="Internal").ap()
    y_dram = nc.dram_tensor("y_dram", [MAX_BLOCKS * BLOCK, D], F32, kind="Internal").ap()
    x_units = x.rearrange("(u j p) d -> u p j d", p=P, j=UT)
    xn_units = xn_dram.rearrange("(u j p) d -> u p j d", p=P, j=UT)
    out_units = out.rearrange("(u j p) d -> u p j d", p=P, j=UT)
    y_halves = y_dram.rearrange("(n s p) d -> n p s d", p=P, s=SUBS)

    with ExitStack() as ctx:
        def sb(name, shape, dt=F32, to=ctx):
            return to.enter_context(nc.sbuf_tensor(name, shape, dt))

        def sem(name):
            return ctx.enter_context(nc.semaphore(name))

        psum = ctx.enter_context(nc.psum_tensor("psum", [P, 8, 512], F32))
        bank = [psum[:, i, :] for i in range(8)]
        squares_ps = psum[:, 5:7, :].rearrange("p b n -> p (b n)")

        x_hi = sb("x_hi", [P, T], F32R)
        x_lo = sb("x_lo", [P, T], F32R)
        keys = sb("keys", [P, T])
        inv_norm = sb("inv_norm", [P, TILES * H])
        ident = sb("ident", [P, P])
        proj_hi = sb("proj_hi", [P, 6, D], F32R)
        proj_lo = sb("proj_lo", [P, 6, D], F32R)
        wo_c = sb("wo_c", [P, D])
        collect = sb("collect", [P, HD, P])
        spread = sb("spread", [P, HD, P], F32R)
        weight1 = sb("weight1", [P, TILES])
        weight2 = sb("weight2", [P, TILES])
        slots_u = sb("slots_u", [P, 2, TILES], U32)
        token_of = sb("token_of", [P, TABLE], U32)
        tokens_now = sb("tokens_now", [P, 2, SUBS], U32)
        slots_now = sb("slots_now", [P, 2, 2, UT], U32)
        starts = sb("starts", [P, E], I32)
        ends = sb("ends", [P, E], I32)
        k_len = sb("k_len", [P, TILES * H])
        eps_col = sb("eps_col", [P, 1])

        early = ExitStack()
        proj_raw = sb("proj_raw", [P, 5, D], to=early)
        wg1_s = sb("wg1_s", [HD, D], to=early)
        wg2t_s = sb("wg2t_s", [HD, D], to=early)
        wot_s = sb("wot_s", [P, D], to=early)
        wo_l = sb("wo_l", [P, D], to=early)
        lnw_s = sb("lnw_s", [P, 1], to=early)
        center = sb("center", [P, P], to=early)
        heads = sb("heads", [P, H], to=early)
        spread_raw = sb("spread_raw", [P, HD, P], to=early)
        logits_t = sb("logits_t", [E, 2, UNIT], to=early)
        zeros = sb("zeros", [P, BLOCK // P, D], to=early)
        x_rows = sb("x_rows", [P, 2, UT, D], to=early)
        xn_rows = sb("xn_rows", [P, 2, UT, D], to=early)
        bn = sb("bn", [P, 2, UT, 6], to=early)
        mean_var = sb("mean_var", [P, 2, UT, 2], to=early)
        std = sb("std", [P, 2, UT], to=early)
        rstd = sb("rstd", [P, 2, UT], to=early)
        k_sq = sb("k_sq", [P, 2, UNIT], to=early)
        ss = sb("ss", [P, TILES * H], to=early)
        bias_g = sb("bias_g", [P, UT, E], to=early)
        rank_c = sb("rank_c", [P, E, TILES], to=early)
        logits = sb("logits", [P, E, TILES], to=early)
        logits2 = sb("logits2", [P, E, TILES], to=early)
        eq1 = sb("eq1", [P, E, TILES], to=early)
        eq2 = sb("eq2", [P, E, TILES], to=early)
        cand1 = sb("cand1", [P, E, TILES], to=early)
        cand2 = sb("cand2", [P, E, TILES], to=early)
        one1 = sb("one1", [P, E, TILES], to=early)
        one2 = sb("one2", [P, E, TILES], to=early)
        chosen = sb("chosen", [P, E, TILES], BF16, to=early)
        top1 = sb("top1", [P, TILES], to=early)
        top2 = sb("top2", [P, TILES], to=early)
        first1 = sb("first1", [P, TILES], to=early)
        first2 = sb("first2", [P, TILES], to=early)
        gap = sb("gap", [P, TILES], to=early)
        e_gap = sb("e_gap", [P, TILES], to=early)
        e_sum = sb("e_sum", [P, TILES], to=early)
        counts = sb("counts", [P, E, TILES], to=early)
        not_first = sb("not_first", [P, E, TILES], to=early)
        upto = sb("upto", [P, E, TILES], to=early)
        place_a = sb("place_a", [P, E, TILES], to=early)
        place_b = sb("place_b", [P, E, TILES], to=early)
        place = sb("place", [P, E, TILES], to=early)
        over = sb("over", [P, E, T // BLOCK], to=early)
        blocks_of = sb("blocks_of", [P, E], to=early)
        blocks_min = sb("blocks_min", [P, E], to=early)
        ones_e = sb("ones_e", [P, E], to=early)
        end_f = sb("end_f", [P, E], to=early)
        start_f = sb("start_f", [P, E], to=early)
        picked1 = sb("picked1", [P, E, TILES], to=early)
        picked2 = sb("picked2", [P, E, TILES], to=early)
        slots_f = sb("slots_f", [P, 2, TILES], to=early)
        row_u = sb("row_u", [P, 2, TILES], U32, to=early)
        tile_u = sb("tile_u", [P, 2, TILES], U32, to=early)
        row_f = sb("row_f", [P, 2, TILES], to=early)
        tile_f = sb("tile_f", [P, 2, TILES], to=early)
        iota_raw = sb("iota_raw", [P, TABLE], to=early)
        iota = sb("iota", [P, TABLE], BF16, to=early)
        token_c = sb("token_c", [P, 1 + TILES], to=early)
        below_raw = sb("below_raw", [P, P], to=early)
        below = sb("below", [P, P], BF16, to=early)
        ones_b = sb("ones_b", [P, P], BF16, to=early)
        zero_b = sb("zero_b", [P, TABLE], BF16, to=early)
        is_row = sb("is_row", [P, 4, P], BF16, to=early)
        is_tile_p = sb("is_tile_p", [P, 4, TABLE], BF16, to=early)
        is_tile_t = sb("is_tile_t", [P, 4, TABLE], BF16, to=early)
        early.close()

        mid = ExitStack()
        w_raw = sb("w_raw", [P, 2, 2, HID], to=mid)
        w_hi = sb("w_hi", [P, 2, 2, HID], F32R, to=mid)
        w_lo = sb("w_lo", [P, 2, 2, HID], F32R, to=mid)
        w2_s = sb("w2_s", [P, 2, HC, D], to=mid)
        b0_s = sb("b0_s", [P, E * HC], to=mid)
        b1_s = sb("b1_s", [P, E * HC], to=mid)
        b2_s = sb("b2_s", [P, E * D], to=mid)
        slot_rows = sb("slot_rows", [P, 2, SUBS, D], to=mid)
        xs_hi = sb("xs_hi", [P, 2, HALF], F32R, to=mid)
        xs_lo = sb("xs_lo", [P, 2, HALF], F32R, to=mid)
        gated = sb("gated", [P, 2, HALF], to=mid)
        hidden = sb("hidden", [P, 2, HC, HALF], to=mid)
        y_rows = sb("y_rows", [P, 2, SUBS, D], to=mid)
        mid.close()

        late = ExitStack()
        q_s = sb("q_s", [P, 2, UNIT], to=late)
        v_s = sb("v_s", [P, 2, UNIT], to=late)
        v_hi = sb("v_hi", [P, 2, UNIT], F32R, to=late)
        v_lo = sb("v_lo", [P, 2, UNIT], F32R, to=late)
        decay_t = sb("decay_t", [P, UNIT], to=late)
        decay = sb("decay", [P, 2, UNIT], to=late)
        gate_t = sb("gate_t", [P, 2, UNIT], to=late)
        k_n = sb("k_n", [P, 2, UNIT], to=late)
        kv = sb("kv", [P, 2, UNIT], to=late)
        state = sb("state", [P, 4, UNIT], to=late)
        q_state = sb("q_state", [P, 4, UNIT], to=late)
        o_s = sb("o_s", [P, 2, UNIT], to=late)
        bn_o = sb("bn_o", [P, UT, 6], to=late)
        mv_o = sb("mv_o", [P, 2, UT, 2], to=late)
        std_o = sb("std_o", [P, 2, UT], to=late)
        rstd_o = sb("rstd_o", [P, 2, UT], to=late)
        x_res = sb("x_res", [P, 2, UT, D], to=late)
        y1 = sb("y1", [P, 2, UT, D], to=late)
        y2 = sb("y2", [P, 2, UT, D], to=late)
        y12 = sb("y12", [P, 2, UT, D], to=late)
        attn_x = sb("attn_x", [P, 2, UT, D], to=late)
        out_s = sb("out_s", [P, 2, UT, D], to=late)
        inv_u = sb("inv_u", [P, 2, UT * H, HD], to=late)
        late.close()

        consts_in = sem("consts_in")
        stood = sem("stood")
        early_consts = sem("early_consts")
        x_in = [sem("x_in0"), sem("x_in1")]
        bn_ready = sem("bn_ready")
        stats_ready = sem("stats_ready")
        std_ready = sem("std_ready")
        rstd_ready = sem("rstd_ready")
        xn_ready = sem("xn_ready")
        xn_out = [sem("xn_out0"), sem("xn_out1")]
        turned = sem("turned")
        hi_ready = sem("hi_ready")
        lo_ready = sem("lo_ready")
        logits_t_done = sem("logits_t_done")
        logits_t_ready = sem("logits_t_ready")
        logits_done = sem("logits_done")
        logits_ready = sem("logits_ready")
        zeros_ready = sem("zeros_ready")
        zeros_out = sem("zeros_out")
        rows_stored = sem("rows_stored")
        fold_ps = sem("fold_ps")
        fold = sem("fold")
        g_hi_ready = sem("g_hi_ready")
        folded = sem("folded")
        k_done = sem("k_done")
        k_ready = sem("k_ready")
        sq_ready = sem("sq_ready")
        ss_done = sem("ss_done")
        ss_ready = sem("ss_ready")
        len_ready = sem("len_ready")
        route = sem("route")
        gap_ready = sem("gap_ready")
        gap_exp = sem("gap_exp")
        chosen_ready = sem("chosen_ready")
        counts_done = sem("counts_done")
        onehot_ready = sem("onehot_ready")
        onehot_used = sem("onehot_used")
        table_done = sem("table_done")
        routed = sem("routed")
        raw_in = [sem("raw_in0"), sem("raw_in1")]
        w2_in = [sem("w2_in0"), sem("w2_in1")]
        bias_in = sem("bias_in")
        w_hi_ready = sem("w_hi_ready")
        w_split = sem("w_split")
        inv_ready = sem("inv_ready")
        rows_in = [sem("rows_in0"), sem("rows_in1")]
        xs_turned = sem("xs_turned")
        tokens_ready = sem("tokens_ready")
        slots_ready = sem("slots_ready")
        xs_hi_ready = sem("xs_hi_ready")
        xs_ready = sem("xs_ready")
        g_done = sem("g_done")
        h_done = sem("h_done")
        gated_ready = sem("gated_ready")
        hidden_ready = sem("hidden_ready")
        down_done = sem("down_done")
        y_ready = sem("y_ready")
        y_out = [sem("y_out0"), sem("y_out1")]
        experts_over = sem("experts_over")
        proj_done = sem("proj_done")
        proj_read = sem("proj_read")
        v_hi_ready = sem("v_hi_ready")
        v_lo_ready = sem("v_lo_ready")
        decay_ready = sem("decay_ready")
        decay_reset = sem("decay_reset")
        inv_ready_u = sem("inv_ready_u")
        inv_turned = sem("inv_turned")
        kn_ready = sem("kn_ready")
        spread_done = sem("spread_done")
        kv_ready = sem("kv_ready")
        state_ready = sem("state_ready")
        qs_pool = sem("qs_pool")
        qs_dve = sem("qs_dve")
        collected = sem("collected")
        o_ready = sem("o_ready")
        o_turned = sem("o_turned")
        out_done = sem("out_done")
        bn_o_ready = sem("bn_o_ready")
        var_ready = sem("var_ready")
        std_o_ready = sem("std_o_ready")
        rstd_o_ready = sem("rstd_o_ready")
        res_in = [sem("res_in0"), sem("res_in1")]
        y_in = [sem("y_in0"), sem("y_in1")]
        y_scaled = sem("y_scaled")
        y12_ready = sem("y12_ready")
        attn_x_ready = sem("attn_x_ready")
        sum_ready = sem("sum_ready")
        out_out = [sem("out_out0"), sem("out_out1")]


        EARLY_LOADS = [(ident, ident_in), (proj_raw, w_proj), (wg1_s, wg1), (wg2t_s, wg2t),
                       (wot_s, wot), (lnw_s, ln_w), (center, center_in), (heads, heads_in),
                       (spread_raw, spread_in), (collect, collect_in), (bias_g, gate_b), (rank_c, rank_in),
                       (iota_raw, iota_in), (token_c, token_in), (below_raw, below_in)]

        def wait(eng, semaphore, value):
            if not (isinstance(value, int) and value <= 0):
                eng.wait_ge(semaphore, value)

        def stand_apart(eng):
            eng.sem_inc(stood, 1)

        def units_in_pairs(eng, body):
            for u in range(4):
                body(u, u % 2, u // 2)
            with eng.Fori(2, UNITS // 2) as i:
                body(2 * i, 0, i)
                body(2 * i + 1, 1, i)

        def units_in_steps(eng, step):
            for u in range(3):
                step(u, u % 2, u // 2, u == 0, False)
            with eng.Fori(1, UNITS // 2 - 1) as i:
                step(2 * i + 1, 1, i, False, False)
                step(2 * i + 2, 0, i + 1, False, False)
            step(UNITS - 1, 1, UNITS // 2 - 1, False, True)

        def block_range(eng, e):
            start = eng.value_load(starts[0:1, bass.ds(e, 1)], min_val=0, max_val=MAX_BLOCKS)
            end = eng.value_load(ends[0:1, bass.ds(e, 1)], min_val=1, max_val=MAX_BLOCKS)
            return start, end

        def all_blocks(eng):
            return eng.value_load(ends[0:1, E - 1:E], min_val=1, max_val=MAX_BLOCKS)

        def one(view, i):
            if isinstance(i, int):
                return view[i]
            if len(view.shape) == 4:
                return view[bass.ds(i, 1)].rearrange("u p j d -> (u p) j d")
            return view[bass.ds(i, 1)].rearrange("u p d -> (u p) d")

        block = ctx.enter_context(nc.Block())

        @block.sync
        def _(sp):
            def load_x(u, par):
                sp.dma_start(x_rows[:, par], one(x_units, u)).then_inc(x_in[par], 16)

            load_x(0, 0)
            load_x(1, 1)
            for dst, src in EARLY_LOADS:
                sp.dma_start(dst[:], src).then_inc(consts_in, 16)

            sp.wait_ge(zeros_ready, 1)
            for b in range(MIN_BLOCKS, MAX_BLOCKS):
                sp.dma_start(y_dram[BLOCK * b:BLOCK * b + BLOCK].rearrange("(j p) d -> p j d", p=P), zeros[:]
                             ).then_inc(zeros_out, 16)

            def pass_rows(u, par, k):
                sp.wait_ge(xn_ready, UT * (u + 1))
                sp.dma_start(one(xn_units, u), xn_rows[:, par]).then_inc(xn_out[par], 16)
                load_x((u + 2) % UNITS, par)

            units_in_pairs(sp, pass_rows)
            for par in range(2):
                sp.wait_ge(x_in[par], 16 * (UNITS // 2 + 1))
                sp.wait_ge(xn_out[par], 16 * (UNITS // 2))
            sp.wait_ge(zeros_out, 16 * (MAX_BLOCKS - MIN_BLOCKS))
            sp.sem_inc(rows_stored, 1)

            def load_raw(e, par):
                sp.dma_start(w_raw[:, par, 0], one(w0, e)).then_inc(raw_in[par], 16)
                sp.dma_start(w_raw[:, par, 1], one(w1, e)).then_inc(raw_in[par], 16)

            def load_w2(e, par):
                sp.dma_start(w2_s[:, par], one(w2, e)).then_inc(w2_in[par], 16)

            sp.wait_ge(routed, 1)
            sp.wait_ge(len_ready, 1)
            load_raw(0, 0)
            load_w2(0, 0)
            for dst, src in ((b0_s, b0), (b1_s, b1), (b2_s, b2)):
                sp.dma_start(dst[:], src).then_inc(bias_in, 16)
            load_raw(1, 1)
            for h in range(2):
                sp.sem_inc(y_out[h], 16)
            with sp.Fori(0, E // 2) as pair:
                for ep in range(2):
                    e = 2 * pair + ep
                    start, end = block_range(sp, e)
                    sp.wait_ge(down_done, 2 * start + 2)
                    load_w2((e + 1) % E, 1 - ep)
                    sp.wait_ge(w_split, e + 1)
                    load_raw((e + 2) % E, ep)
                    with sp.Fori(start, end) as b:
                        for h in range(2):
                            sp.wait_ge(y_ready, 2 * b + h + 3)
                            sp.dma_start(one(y_halves, 2 * b + h), y_rows[:, h]).then_inc(y_out[h], 16)
            total = all_blocks(sp)
            for h in range(2):
                sp.wait_ge(y_out[h], 16 * total + 16)
                sp.wait_ge(raw_in[h], 32 * (E // 2 + 1))
                sp.wait_ge(rows_in[h], 32 * total + 32)
            sp.wait_ge(w2_in[0], 16 * (E // 2 + 1))
            sp.wait_ge(w_split, E + 1)
            sp.wait_ge(xs_ready, 2 * total + 2)
            sp.sem_inc(experts_over, 1)

            def load_res(u, par):
                wait(sp, attn_x_ready, UT * (u - 1))
                sp.dma_start(x_res[:, par], one(x_units, u)).then_inc(res_in[par], 16)

            def store(u, par):
                sp.wait_ge(sum_ready, u + 1)
                sp.dma_start(one(out_units, u), out_s[:, par]).then_inc(out_out[par], 16)

            load_res(0, 0)
            load_res(1, 1)
            with sp.Fori(0, UNITS // 2 - 1) as i:
                for par in range(2):
                    store(2 * i + par, par)
                    load_res(2 * i + par + 2, par)
            store(UNITS - 2, 0)
            store(UNITS - 1, 1)
            for par in range(2):
                sp.wait_ge(out_out[par], 16 * (UNITS // 2))

        @block.gpsimd
        def _(pool):
            def norm_rows(u, par, k):
                pool.wait_ge(rstd_ready, u + 1)
                wait(pool, turned, u - 1)
                wait(pool, xn_out[par], 16 * k)
                stand_apart(pool)
                for j in range(UT):
                    pool.tensor_scalar(xn_rows[:, par, j], x_rows[:, par, j], mean_var[:, par, j, 0:1],
                                       rstd[:, par, j:j + 1], ALU.subtract, ALU.mult).then_inc(xn_ready, 1)

            units_in_pairs(pool, norm_rows)

            pool.wait_ge(routed, 1)
            pool.wait_ge(len_ready, 1)
            pool.wait_ge(rows_stored, 1)
            total = all_blocks(pool)
            with pool.Fori(0, total + 1) as b:
                for h in range(2):
                    pool.wait_ge(xs_turned, 2 * b + h + 1)
                    at = bass.ds((2 * b + h) * SUBS, SUBS)
                    pool.tensor_copy(tokens_now[:, h], token_of[:, at]).then_inc(tokens_ready, 1)
                    pool.wait_ge(tokens_ready, 2 * b + h + 1)
                    stand_apart(pool)
                    for s in range(SUBS):
                        pool.indirect_dma_start(slot_rows[:, h, s], None, xn_dram,
                                                bass.IndirectOffsetOnAxis(tokens_now[:, h, s:s + 1], 0)
                                                ).then_inc(rows_in[h], 16)

            pool.wait_ge(experts_over, 1)

            def add_rows(u, par):
                pool.wait_ge(y_scaled, 2 * UT * (u + 1))
                wait(pool, sum_ready, u - 1)
                pool.tensor_tensor(y12[:, par], y1[:, par], y2[:, par], ALU.add).then_inc(y12_ready, 1)

            def step(u, par, k, first, last):
                wait(pool, y12_ready, u - 1)
                pool.tensor_copy(slots_now[:, par], slots_u[:, :, bass.ds(UT * u, UT)]).then_inc(slots_ready, 1)
                pool.wait_ge(slots_ready, u + 1)
                for n, v in enumerate(POOL_V):
                    pool.wait_ge(state_ready, HD * u + v + 1)
                    wait(pool, collected, HD * u + v - 3)
                    pool.tensor_tensor(q_state[:, v % 4], state[:, v % 4], q_s[:, par], ALU.mult
                                       ).then_inc(qs_pool, 1)
                    for choice, rows in ((0, y1), (1, y2)):
                        pool.indirect_dma_start(
                            rows[:, par, n], None, y_dram,
                            bass.IndirectOffsetOnAxis(slots_now[:, par, choice, n:n + 1], 0),
                        ).then_inc(y_in[par], 16)
                if not first:
                    add_rows(u - 1, 1 - par)

            assert len(POOL_V) == UT
            units_in_steps(pool, step)
            add_rows(UNITS - 1, 1)

        @block.scalar
        def _(act):
            act.wait_ge(early_consts, 1)

            def stds_and_high_part(u, par, k):
                act.wait_ge(stats_ready, UT * (u + 1))
                wait(act, rstd_ready, u - 1)
                act.activation(std[:, par], mean_var[:, par, :, 1], ACT.Sqrt, bias=eps_col[:, 0:1]
                               ).then_inc(std_ready, 1)
                act.wait_ge(turned, u + 1)
                stand_apart(act)
                act.activation(x_hi[:, bass.ds(UNIT * u, UNIT)], bank[par][:, :], ACT.Copy).then_inc(hi_ready, 1)
                if not (isinstance(u, int) and u == 0):
                    logits_row(u - 1, 1 - par)

            def logits_row(u, par):
                act.wait_ge(logits_t_done, u + 1)
                wait(act, logits_done, u - 1)
                act.activation(logits_t[:, par], bank[2 + par][0:E, :], ACT.Copy).then_inc(logits_t_ready, 1)

            units_in_pairs(act, stds_and_high_part)
            logits_row(UNITS - 1, 1)

            def key_unit(u, par, k):
                act.wait_ge(k_done, u + 1)
                stand_apart(act)
                act.activation(keys[:, bass.ds(UNIT * u, UNIT)], bank[3 + par][:, :], ACT.Silu).then_inc(k_ready, 1)
                act.wait_ge(k_ready, u + 1)
                wait(act, ss_done, u - 1)
                stand_apart(act)
                act.activation(k_sq[:, par], keys[:, bass.ds(UNIT * u, UNIT)], ACT.Square).then_inc(sq_ready, 1)

            act.wait_ge(gap_ready, 1)
            act.activation(e_gap[:], gap[:], ACT.Exp).then_inc(gap_exp, 1)
            units_in_pairs(act, key_unit)
            act.wait_ge(ss_ready, 2)
            act.activation(k_len[:], ss[:], ACT.Sqrt).then_inc(len_ready, 1)

            act.wait_ge(routed, 1)
            act.wait_ge(bias_in, 48)

            def xs_high_part(n, h):
                act.wait_ge(xs_turned, n + 3)
                act.activation(xs_hi[:, h], bank[6 + h][:, 0:HALF], ACT.Copy).then_inc(xs_hi_ready, 1)

            for h in range(2):
                xs_high_part(h, h)
            with act.Fori(0, E // 2) as pair:
                for ep in range(2):
                    e = 2 * pair + ep
                    start, end = block_range(act, e)
                    with act.Fori(start, end) as b:
                        for h in range(2):
                            for c in range(HC):
                                n = (2 * b + h) * HC + c
                                act.wait_ge(g_done, n + 1)
                                act.wait_ge(hidden_ready, n + 1)
                                stand_apart(act)
                                act.activation(gated[:, c % 2], bank[2 + c % 2][:, 0:HALF], ACT.Silu,
                                               bias=b1_s[:, bass.ds(HC * e + c, 1)]).then_inc(gated_ready, 1)
                        for h in range(2):
                            xs_high_part(2 * b + 2 + h, h)

            act.wait_ge(experts_over, 1)

            def head(u, par):
                wait(act, o_ready, u - 1)
                stand_apart(act)
                act.activation(inv_u[:, par], inv_norm[:, bass.ds(UT * H * u, UT * H)].unsqueeze(2)
                               .broadcast_to([P, UT * H, HD]), ACT.Copy).then_inc(inv_ready_u, 1)
                act.wait_ge(proj_done, 4 * u + 1)
                act.activation(q_s[:, par], bank[0][:, :], ACT.Silu).then_inc(proj_read, 1)
                act.wait_ge(proj_done, 4 * u + 2)
                act.activation(v_s[:, par], bank[1][:, :], ACT.Silu).then_inc(proj_read, 1)
                act.wait_ge(proj_read, 4 * u + 2)
                act.activation(v_hi[:, par], v_s[:, par], ACT.Copy).then_inc(v_hi_ready, 1)
                act.wait_ge(proj_done, 4 * u + 3)
                wait(act, decay_ready, u)
                act.activation(decay_t[:], bank[0][:, :], ACT.Tanh, scale=0.5).then_inc(proj_read, 1)
                act.wait_ge(proj_done, 4 * u + 4)
                act.activation(gate_t[:, par], bank[1][:, :], ACT.Tanh, scale=0.5).then_inc(proj_read, 1)
                act.wait_ge(proj_read, 4 * u + 3)
                act.activation(decay[:, par], decay_t[:], ACT.Copy, scale=0.5, bias=0.5).then_inc(decay_ready, 1)

            def tail(u, par, k):
                act.wait_ge(var_ready, UT * (u + 1))
                wait(act, rstd_o_ready, u - 1)
                act.activation(std_o[:, par], mv_o[:, par, :, 1], ACT.Sqrt, bias=eps_col[:, 0:1]
                               ).then_inc(std_o_ready, 1)
                act.wait_ge(y_in[par], 16 * 2 * UT * (k + 1))
                stand_apart(act)
                for j in range(UT):
                    for rows, weight in ((y1, weight1), (y2, weight2)):
                        act.activation(rows[:, par, j], rows[:, par, j], ACT.Copy,
                                       scale=weight[:, bass.ds(UT * u + j, 1)]).then_inc(y_scaled, 1)

            head(0, 0)

            def step(u, par, k, first, last):
                if not first:
                    tail(u - 1, 1 - par, k if par else k - 1)
                if not last:
                    head(u + 1, 1 - par)

            units_in_steps(act, step)
            tail(UNITS - 1, 1, UNITS // 2 - 1)

        @block.vector
        def _(dve):
            sub, mul, add = ALU.subtract, ALU.mult, ALU.add
            n_fold = [0]

            def did(ins):
                n_fold[0] += 1
                return ins.then_inc(fold, 1)

            dve.memset(eps_col[:], EPS).then_inc(early_consts, 1)
            dve.memset(zeros[:], 0.0).then_inc(zeros_ready, 1)
            dve.wait_ge(consts_in, 16 * len(EARLY_LOADS))
            did(dve.tensor_copy(proj_hi[:, 0:G], proj_raw[:]))
            dve.wait_ge(fold, 1)
            did(dve.tensor_tensor(proj_lo[:, 0:G], proj_raw[:], proj_hi[:, 0:G].bitcast(F32), sub))
            did(dve.tensor_scalar(wo_l[:], wot_s[:], lnw_s[:, 0:1], None, mul))
            for v in range(HD):
                did(dve.tensor_copy(spread[:, v], spread_raw[:, v]))
            did(dve.tensor_copy(iota[:], iota_raw[:]))
            did(dve.tensor_copy(below[:], below_raw[:]))
            did(dve.memset(ones_b[:], 1.0))
            did(dve.memset(zero_b[:], 0.0))
            did(dve.memset(ones_e[:], 1.0))
            did(dve.memset(not_first[:, :, 1:TILES], 1.0))
            did(dve.memset(not_first[:, :, 0:1], 0.0))
            assert n_fold[0] == FOLD
            dve.wait_ge(fold_ps, 2)
            dve.tensor_copy(proj_hi[:, G], bank[7][:, 0:D]).then_inc(g_hi_ready, 1)
            dve.wait_ge(g_hi_ready, 1)
            dve.tensor_tensor(proj_lo[:, G], bank[7][:, 0:D], proj_hi[:, G].bitcast(F32), sub).then_inc(folded, 1)
            dve.tensor_copy(wo_c[:], bank[7][:, D:2 * D]).then_inc(folded, 1)

            def statistics(u, par, k):
                dve.wait_ge(x_in[par], 16 * (k + 1))
                wait(dve, xn_ready, UT * (u - 1))
                for j in range(UT):
                    dve.bn_stats(bn[:, par, j], x_rows[:, par, j]).then_inc(bn_ready, 1)
                dve.wait_ge(bn_ready, UT * (u + 1))
                stand_apart(dve)
                for j in range(UT):
                    dve.bn_aggr(mean_var[:, par, j], bn[:, par, j]).then_inc(stats_ready, 1)

            def low_part(u, par):
                at = bass.ds(UNIT * u, UNIT)
                dve.wait_ge(hi_ready, u + 1)
                dve.tensor_tensor(x_lo[:, at], bank[par][:, :], x_hi[:, at].bitcast(F32), sub).then_inc(lo_ready, 1)

            def take_logits(u, par):
                dve.wait_ge(logits_done, u + 1)
                dve.tensor_tensor(logits[:, :, bass.ds(UT * u, UT)].rearrange("p e j -> p j e"),
                                  bank[4 + par][:, 0:UT * E].rearrange("p (j e) -> p j e", e=E), bias_g[:], add
                                  ).then_inc(logits_ready, 1)

            def norm_unit(u, par, k):
                statistics(u, par, k)
                if not (isinstance(u, int) and u == 0):
                    low_part(u - 1, 1 - par)
                dve.wait_ge(std_ready, u + 1)
                wait(dve, xn_ready, UT * (u - 1))
                dve.reciprocal(rstd[:, par], std[:, par]).then_inc(rstd_ready, 1)
                if not (isinstance(u, int) and u < 2):
                    take_logits(u - 2, par)

            units_in_pairs(dve, norm_unit)
            low_part(UNITS - 1, 1)
            take_logits(UNITS - 2, 0)
            take_logits(UNITS - 1, 1)

            n_route = [0]

            def step_done(ins):
                n_route[0] += 1
                ins.then_inc(route, 1)
                dve.wait_ge(route, n_route[0])

            def over_experts(a):
                return a.unsqueeze(1).broadcast_to([P, E, TILES])

            dve.wait_ge(logits_ready, UNITS)
            source = logits
            for top, eq, cand, first_e, pick in ((top1, eq1, cand1, first1, one1), (top2, eq2, cand2, first2, one2)):
                step_done(dve.tensor_reduce(top[:], source[:].rearrange("p e t -> p t e"), AX.X, ALU.max))
                if source is logits2:
                    step_done(dve.tensor_tensor(gap[:], top2[:], top1[:], sub))
                    dve.sem_inc(gap_ready, 1)
                step_done(dve.tensor_tensor(eq[:], source[:], over_experts(top[:]), ALU.is_equal))
                step_done(dve.tensor_tensor(cand[:], eq[:], rank_c[:], mul))
                step_done(dve.tensor_reduce(first_e[:], cand[:].rearrange("p e t -> p t e"), AX.X, ALU.max))
                step_done(dve.tensor_tensor(pick[:], cand[:], over_experts(first_e[:]), ALU.is_equal))
                if source is logits:
                    step_done(dve.scalar_tensor_tensor(out=logits2[:], in0=pick[:], scalar=-3e38, in1=logits[:],
                                                       op0=mul, op1=add))
                    source = logits2
            dve.tensor_tensor(chosen[:], one1[:], one2[:], add).then_inc(chosen_ready, 1)
            dve.wait_ge(gap_exp, 1)
            step_done(dve.tensor_scalar(e_sum[:], e_gap[:], 1.0, None, add))
            step_done(dve.reciprocal(weight1[:], e_sum[:]))
            step_done(dve.tensor_tensor(weight2[:], e_gap[:], weight1[:], mul))
            dve.wait_ge(counts_done, 1)
            step_done(dve.tensor_copy(counts[:].rearrange("p e t -> p (e t)"), bank[1][:, :]))
            step_done(dve.tensor_tensor_scan(upto[:].rearrange("p e t -> p (e t)"),
                                             not_first[:].rearrange("p e t -> p (e t)"),
                                             counts[:].rearrange("p e t -> p (e t)"), 0.0, mul, add))
            step_done(dve.scalar_tensor_tensor(
                out=over[:], in0=upto[:, :, TILES - 1:TILES].broadcast_to([P, E, T // BLOCK]), scalar=1.0 / BLOCK,
                in1=iota_raw[:, 0:T // BLOCK].unsqueeze(1).broadcast_to([P, E, T // BLOCK]), op0=mul, op1=ALU.is_gt))
            step_done(dve.tensor_reduce(blocks_of[:], over[:], AX.X, add))
            step_done(dve.tensor_scalar(blocks_min[:], blocks_of[:], 1.0, None, ALU.max))
            step_done(dve.tensor_tensor_scan(end_f[:], ones_e[:], blocks_min[:], 0.0, mul, add))
            step_done(dve.tensor_tensor(start_f[:], end_f[:], blocks_min[:], sub))
            step_done(dve.tensor_copy(ends[:], end_f[:]))
            step_done(dve.tensor_copy(starts[:], start_f[:]))
            step_done(dve.tensor_tensor(place_a[:], upto[:], counts[:], sub))
            step_done(dve.tensor_tensor(place_b[:].rearrange("p e t -> p (e t)"), bank[0][:, :],
                                        place_a[:].rearrange("p e t -> p (e t)"), add))
            step_done(dve.scalar_tensor_tensor(out=place[:], in0=start_f[:].unsqueeze(2).broadcast_to([P, E, TILES]),
                                               scalar=float(BLOCK), in1=place_b[:], op0=mul, op1=add))
            for choice, pick, picked in ((0, one1, picked1), (1, one2, picked2)):
                step_done(dve.tensor_tensor(picked[:], pick[:], place[:], mul))
                step_done(dve.tensor_reduce(slots_f[:, choice], picked[:].rearrange("p e t -> p t e"), AX.X, add))
            step_done(dve.tensor_copy(slots_u[:], slots_f[:]))
            step_done(dve.tensor_scalar(row_u[:], slots_u[:], P - 1, None, ALU.bitwise_and))
            step_done(dve.tensor_scalar(tile_u[:], slots_u[:], 7, None, ALU.logical_shift_right))
            step_done(dve.tensor_copy(row_f[:], row_u[:]))
            step_done(dve.tensor_copy(tile_f[:], tile_u[:]))

            def one_hots(u, par, k):
                for m in range(2 * UT):
                    j, choice, buf = m // 2, m % 2, m % 4
                    t = UT * u + j
                    row, tile = (a[:, choice, bass.ds(t, 1)] for a in (row_f, tile_f))
                    wait(dve, onehot_used, 2 * UT * u + m - 3)
                    dve.tensor_scalar(is_row[:, buf], iota[:, 0:P], row, None, ALU.is_equal).then_inc(onehot_ready, 1)
                    dve.tensor_scalar(is_tile_p[:, buf], iota[:], tile, token_c[:, 0:1], ALU.is_equal, mul
                                      ).then_inc(onehot_ready, 1)
                    dve.tensor_scalar(is_tile_t[:, buf], iota[:], tile, token_c[:, bass.ds(t + 1, 1)],
                                      ALU.is_equal, mul).then_inc(onehot_ready, 1)

            units_in_pairs(dve, one_hots)
            dve.wait_ge(ss_done, UNITS)
            for i in range(2):
                dve.tensor_scalar(ss[:, 512 * i:512 * i + 512], bank[5 + i][:, :], NORM_MIN_SQ, None, ALU.max
                                  ).then_inc(ss_ready, 1)
            dve.wait_ge(table_done, 1)
            dve.tensor_copy(token_of[:], bank[7][:, 0:TABLE]).then_inc(routed, 1)

            dve.wait_ge(routed, 1)
            dve.wait_ge(len_ready, 1)
            dve.wait_ge(bias_in, 48)
            dve.sem_inc(hidden_ready, 2)
            dve.sem_inc(y_ready, 2)

            def split_weights(s, par, k):
                dve.wait_ge(raw_in[par], 32 * (k + 1))
                for i in range(2):
                    dve.tensor_copy(w_hi[:, par, i], w_raw[:, par, i]).then_inc(w_hi_ready, 1)
                for i in range(2):
                    dve.wait_ge(w_hi_ready, 2 * s + i + 1)
                    ins = dve.tensor_tensor(w_lo[:, par, i], w_raw[:, par, i], w_hi[:, par, i].bitcast(F32), sub)
                ins.then_inc(w_split, 1)

            def xs_low_part(n, h):
                dve.wait_ge(xs_hi_ready, n + 1)
                dve.tensor_tensor(xs_lo[:, h], bank[6 + h][:, 0:HALF], xs_hi[:, h].bitcast(F32), sub
                                  ).then_inc(xs_ready, 1)

            split_weights(0, 0, 0)
            for h in range(2):
                xs_low_part(h, h)
            with dve.Fori(0, E // 2) as pair:
                for ep in range(2):
                    e = 2 * pair + ep
                    start, end = block_range(dve, e)
                    share = bass.ds(TILES * H // E * e, TILES * H // E)
                    dve.reciprocal(inv_norm[:, share], k_len[:, share]).then_inc(inv_ready, 1)
                    dve.wait_ge(down_done, 2 * start + 2)
                    split_weights(e + 1, 1 - ep, pair + ep)
                    with dve.Fori(start, end) as b:
                        for h in range(2):
                            dve.wait_ge(down_done, 2 * b + h + 1)
                            for c in range(HC):
                                n = (2 * b + h) * HC + c
                                dve.wait_ge(h_done, n + 1)
                                dve.wait_ge(gated_ready, n + 1)
                                dve.scalar_tensor_tensor(out=hidden[:, h, c], in0=bank[c % 2][:, 0:HALF],
                                                         scalar=b0_s[:, bass.ds(HC * e + c, 1)],
                                                         in1=gated[:, c % 2], op0=add, op1=mul
                                                         ).then_inc(hidden_ready, 1)
                        for h in range(2):
                            n = 2 * b + h
                            xs_low_part(n + 2, h)
                            dve.wait_ge(down_done, n + 3)
                            dve.wait_ge(y_out[h], 16 * b + 16)
                            for s in range(SUBS):
                                ins = dve.tensor_tensor(y_rows[:, h, s], bank[4 + h][:, D * s:D * s + D],
                                                        b2_s[:, bass.ds(D * e, D)], add)
                            ins.then_inc(y_ready, 1)

            dve.wait_ge(experts_over, 1)

            def head(u, par):
                wait(dve, o_ready, u - 1)
                dve.wait_ge(decay_ready, u + 1)
                for s in range(UNIT // SEQ):
                    dve.memset(decay[:, par, SEQ * s:SEQ * s + 1], 0.0).then_inc(decay_reset, 1)
                dve.wait_ge(v_hi_ready, u + 1)
                dve.tensor_tensor(v_lo[:, par], v_s[:, par], v_hi[:, par].bitcast(F32), sub).then_inc(v_lo_ready, 1)
                dve.wait_ge(inv_turned, u + 1)
                dve.tensor_tensor(k_n[:, par], bank[7][:, :], keys[:, bass.ds(UNIT * u, UNIT)], mul
                                  ).then_inc(kn_ready, 1)

            def statistics_o(u, par):
                dve.wait_ge(o_turned, u + 1)
                wait(dve, std_o_ready, u - 1)
                wait(dve, var_ready, UT * u)
                for j in range(UT):
                    dve.bn_stats(bn_o[:, j], bank[5][:, D * j:D * j + D]).then_inc(bn_o_ready, 1)
                dve.wait_ge(bn_o_ready, UT * (u + 1))
                stand_apart(dve)
                for j in range(UT):
                    dve.bn_aggr(mv_o[:, par, j], bn_o[:, j]).then_inc(var_ready, 1)

            def sum_up(u, par, k):
                dve.wait_ge(std_o_ready, u + 1)
                dve.reciprocal(rstd_o[:, par], std_o[:, par]).then_inc(rstd_o_ready, 1)
                dve.wait_ge(rstd_o_ready, u + 1)
                dve.wait_ge(out_done, u + 1)
                dve.wait_ge(res_in[par], 16 * (k + 1))
                for j in range(UT):
                    dve.scalar_tensor_tensor(out=attn_x[:, par, j], in0=bank[6][:, D * j:D * j + D],
                                             scalar=rstd_o[:, par, j:j + 1], in1=x_res[:, par, j],
                                             op0=mul, op1=add).then_inc(attn_x_ready, 1)
                dve.wait_ge(attn_x_ready, UT * (u + 1))
                dve.wait_ge(y12_ready, u + 1)
                wait(dve, out_out[par], 16 * k)
                dve.tensor_tensor(out_s[:, par], attn_x[:, par], y12[:, par], add).then_inc(sum_ready, 1)

            def step(u, par, k, first, last):
                dve.wait_ge(decay_reset, 2 * u + 2)
                dve.wait_ge(kn_ready, u + 1)
                n_dve = 0
                for v in range(HD):
                    at = HD * u + v
                    dve.wait_ge(spread_done, at + 1)
                    wait(dve, state_ready, at - 1)
                    dve.tensor_tensor(kv[:, v % 2], bank[2 + v % 2][:, :], k_n[:, par], mul).then_inc(kv_ready, 1)
                    dve.wait_ge(kv_ready, at + 1)
                    wait(dve, collected, at - 3)
                    dve.tensor_tensor_scan(state[:, v % 4], decay[:, par], kv[:, v % 2], 0.0, mul, add
                                           ).then_inc(state_ready, 1)
                    if v in DVE_V:
                        dve.wait_ge(state_ready, at + 1)
                        dve.tensor_tensor(q_state[:, v % 4], state[:, v % 4], q_s[:, par], mul).then_inc(qs_dve, 1)
                    if v == HD // 2 and not first:
                        statistics_o(u - 1, 1 - par)
                dve.wait_ge(collected, HD * u + HD)
                dve.scalar_tensor_tensor(out=o_s[:, par], in0=gate_t[:, par], scalar=1.0, in1=bank[4][:, :],
                                         op0=add, op1=mul).then_inc(o_ready, 1)
                if not last:
                    head(u + 1, 1 - par)
                if not first:
                    sum_up(u - 1, 1 - par, k if par else k - 1)

            head(0, 0)
            units_in_steps(dve, step)
            statistics_o(UNITS - 1, 1)
            sum_up(UNITS - 1, 1, UNITS // 2 - 1)

        @block.tensor
        def _(pe):
            def product3(out_ps, w_h, w_l, x_h, x_l):
                pe.matmul(out_ps, w_h, x_h, start=True, stop=False)
                pe.matmul(out_ps, w_h, x_l, start=False, stop=False)
                return pe.matmul(out_ps, w_l, x_h, start=False, stop=True)

            pe.wait_ge(consts_in, 16 * len(EARLY_LOADS))
            pe.wait_ge(fold, FOLD)
            pe.matmul(bank[7][:, 0:D], wg1_s[:], wg2t_s[:], start=True, stop=True).then_inc(fold_ps, 1)
            pe.matmul(bank[7][:, D:2 * D], center[:], wo_l[:], start=True, stop=True).then_inc(fold_ps, 1)

            def unit_product(out_ps, which, u):
                at = bass.ds(UNIT * u, UNIT)
                return product3(out_ps, proj_hi[:, which], proj_lo[:, which], x_hi[:, at], x_lo[:, at])

            def logits_columns(u, par):
                pe.wait_ge(lo_ready, u + 1)
                wait(pe, logits_t_ready, u - 1)
                unit_product(bank[2 + par], L, u).then_inc(logits_t_done, 1)

            def logits_back(u, par):
                pe.wait_ge(logits_t_ready, u + 1)
                wait(pe, logits_ready, u - 1)
                stand_apart(pe)
                for j in range(UT):
                    ins = pe.transpose(bank[4 + par][:, E * j:E * j + E], logits_t[:, par, P * j:P * j + P],
                                       ident[0:E, 0:E])
                ins.then_inc(logits_done, 1)

            def turn_rows(u, par, k):
                pe.wait_ge(xn_ready, UT * (u + 1))
                wait(pe, lo_ready, u - 1)
                for j in range(UT):
                    ins = pe.transpose(bank[par][:, P * j:P * j + P], xn_rows[:, par, j], ident[:])
                ins.then_inc(turned, 1)
                if not (isinstance(u, int) and u == 0):
                    logits_columns(u - 1, 1 - par)
                if not (isinstance(u, int) and u < 2):
                    logits_back(u - 2, par)

            units_in_pairs(pe, turn_rows)
            logits_columns(UNITS - 1, 1)
            logits_back(UNITS - 2, 0)
            logits_back(UNITS - 1, 1)

            pe.wait_ge(chosen_ready, 1)
            chosen_flat = chosen[:].rearrange("p e t -> p (e t)")
            pe.matmul(bank[0], below[:], chosen_flat, start=True, stop=True)
            pe.matmul(bank[1], ones_b[:], chosen_flat, start=True, stop=True).then_inc(counts_done, 1)
            pe.wait_ge(folded, 2)
            table_ps = bank[7][:, 0:TABLE]
            pe.matmul(table_ps, zero_b[:, 0:P], zero_b[:], start=True, stop=False)

            def sums_of_squares(u, par):
                pe.wait_ge(sq_ready, u + 1)
                for j in range(UT):
                    ins = pe.matmul(squares_ps[:, bass.ds(H * (UT * u + j), H)], k_sq[:, par, P * j:P * j + P],
                                    heads[:], start=True, stop=True)
                ins.then_inc(ss_done, 1)

            def keys_and_table(u, par, k):
                wait(pe, k_ready, u - 1)
                unit_product(bank[3 + par], K, u).then_inc(k_done, 1)
                if not (isinstance(u, int) and u == 0):
                    sums_of_squares(u - 1, 1 - par)
                for m in range(2 * UT):
                    pe.wait_ge(onehot_ready, 3 * (2 * UT * u + m + 1))
                    pe.matmul(table_ps, is_row[:, m % 4], is_tile_p[:, m % 4], start=False, stop=False)
                    pe.matmul(table_ps, is_row[:, m % 4], is_tile_t[:, m % 4], start=False, stop=False
                              ).then_inc(onehot_used, 1)

            units_in_pairs(pe, keys_and_table)
            pe.matmul(table_ps, zero_b[:, 0:P], zero_b[:], start=False, stop=True).then_inc(table_done, 1)
            sums_of_squares(UNITS - 1, 1)

            pe.wait_ge(routed, 1)
            pe.wait_ge(len_ready, 1)
            pe.sem_inc(xs_turned, 2)
            pe.sem_inc(down_done, 2)

            def turn_slots(b, h):
                pe.wait_ge(rows_in[h], 32 * b + 32)
                for s in range(SUBS):
                    ins = pe.transpose(bank[6 + h][:, P * s:P * s + P], slot_rows[:, h, s], ident[:])
                ins.then_inc(xs_turned, 1)

            def up(b, h, ep):
                pe.wait_ge(xs_ready, 2 * b + h + 1)
                for c in range(HC):
                    n = (2 * b + h) * HC + c
                    pe.wait_ge(hidden_ready, n + 1)
                    for which, out_ps, done in ((1, bank[2 + c % 2], g_done), (0, bank[c % 2], h_done)):
                        cols = slice(P * c, P * c + P)
                        product3(out_ps[:, 0:HALF], w_hi[:, ep, which, cols], w_lo[:, ep, which, cols],
                                 xs_hi[:, h], xs_lo[:, h]).then_inc(done, 1)

            def down(b, h, ep):
                n = 2 * b + h
                pe.wait_ge(hidden_ready, HC * n + HC + 2)
                pe.wait_ge(y_ready, n + 1)
                for s in range(SUBS):
                    for c in range(HC):
                        ins = pe.matmul(bank[4 + h][:, D * s:D * s + D], hidden[:, h, c, P * s:P * s + P],
                                        w2_s[:, ep, c], start=(c == 0), stop=(c == HC - 1))
                ins.then_inc(down_done, 1)

            for h in range(2):
                turn_slots(0, h)
            with pe.Fori(0, E // 2) as pair:
                for ep in range(2):
                    e = 2 * pair + ep
                    start, end = block_range(pe, e)
                    pe.wait_ge(w_split, e + 1)
                    pe.wait_ge(w2_in[ep], 16 * pair + 16)
                    stand_apart(pe)
                    with pe.Fori(start, end) as b:
                        up(b, 0, ep)
                        up(b, 1, ep)
                        turn_slots(b + 1, 0)
                        down(b, 0, ep)
                        turn_slots(b + 1, 1)
                        down(b, 1, ep)

            pe.wait_ge(experts_over, 1)

            def head(u, par):
                for i, which in enumerate((Q, V, F, G)):
                    wait(pe, proj_read, 4 * u + i - 1)
                    unit_product(bank[i % 2], which, u).then_inc(proj_done, 1)
                pe.wait_ge(inv_ready_u, u + 1)
                wait(pe, kn_ready, u)
                for j in range(UT):
                    rows = inv_u[:, par, H * j:H * j + H].rearrange("p h k -> p (h k)")
                    ins = pe.transpose(bank[7][:, P * j:P * j + P], rows, ident[:])
                ins.then_inc(inv_turned, 1)

            def spread_v(u, par, v):
                if v == 0:
                    pe.wait_ge(v_lo_ready, u + 1)
                wait(pe, kv_ready, HD * u + v - 1)
                pe.matmul(bank[2 + v % 2], spread[:, v], v_hi[:, par], start=True, stop=False)
                pe.matmul(bank[2 + v % 2], spread[:, v], v_lo[:, par], start=False, stop=True
                          ).then_inc(spread_done, 1)

            def collect_v(u, v):
                if v in POOL_V:
                    pe.wait_ge(qs_pool, len(POOL_V) * u + POOL_V.index(v) + 1)
                else:
                    pe.wait_ge(qs_dve, len(DVE_V) * u + DVE_V.index(v) + 1)
                if v == 0:
                    wait(pe, o_ready, u)
                pe.matmul(bank[4], collect[:, v], q_state[:, v % 4], start=(v == 0), stop=(v == HD - 1)
                          ).then_inc(collected, 1)

            def tail(u, par):
                pe.wait_ge(o_ready, u + 1)
                wait(pe, var_ready, UT * u)
                for j in range(UT):
                    ins = pe.transpose(bank[5][:, D * j:D * j + D], o_s[:, par, P * j:P * j + P], ident[:])
                ins.then_inc(o_turned, 1)
                wait(pe, attn_x_ready, UT * u)
                for j in range(UT):
                    ins = pe.matmul(bank[6][:, D * j:D * j + D], o_s[:, par, P * j:P * j + P], wo_c[:],
                                    start=True, stop=True)
                ins.then_inc(out_done, 1)

            def step(u, par, k, first, last):
                spread_v(u, par, 0)
                spread_v(u, par, 1)
                for v in range(HD):
                    collect_v(u, v)
                    if v + 2 < HD:
                        spread_v(u, par, v + 2)
                if not last:
                    head(u + 1, 1 - par)
                tail(u, par)

            head(0, 0)
            units_in_steps(pe, step)


def kernel(L0_attn_x, L0_attn_Wq, L0_attn_Wk, L0_attn_Wv, L0_attn_Wf, L0_attn_Wg1, L0_attn_Wg2, L0_attn_ln_w,
           L0_attn_Wo, L0_ffn_Wg, L0_ffn_bg, L0_ffn_W0, L0_ffn_b0, L0_ffn_W1, L0_ffn_b1, L0_ffn_W2, L0_ffn_b2):
    import concourse.bacc as bacc
    from concourse.bass_utils import run_bass_kernel_spmd

    f32 = np.float32
    a = {k: np.asarray(v) for k, v in dict(
        x=L0_attn_x, Wq=L0_attn_Wq, Wk=L0_attn_Wk, Wv=L0_attn_Wv, Wf=L0_attn_Wf, Wg1=L0_attn_Wg1, Wg2=L0_attn_Wg2,
        ln_w=L0_attn_ln_w, Wo=L0_attn_Wo, Wg=L0_ffn_Wg, bg=L0_ffn_bg, W0=L0_ffn_W0, b0=L0_ffn_b0, W1=L0_ffn_W1,
        b1=L0_ffn_b1, W2=L0_ffn_W2, b2=L0_ffn_b2).items()}
    w_proj = np.zeros((D, 5, D), f32)
    w_proj[:, 0] = a["Wq"].T
    w_proj[:, 1] = a["Wk"].T
    w_proj[:, 2] = a["Wv"].T
    w_proj[:, 3] = np.repeat(a["Wf"].T, HD, axis=1)
    w_proj[:, 4, :E] = a["Wg"]
    row, col = np.arange(P)[:, None], np.arange(P)[None, :]
    spread = np.stack([(row == (col // HD) * HD + v) for v in range(HD)], axis=1).astype(f32)
    collect = np.stack([(row // HD == col // HD) & (col % HD == v) for v in range(HD)], axis=1).astype(f32) * f32(0.5)
    token = np.concatenate([row, np.broadcast_to(P * np.arange(TILES)[None, :], (P, TILES))], axis=1)
    arrays = dict(
        x=a["x"].reshape(T, D),
        w_proj=w_proj,
        wg1=a["Wg1"],
        wg2t=a["Wg2"].T,
        wot=a["Wo"].T,
        ln_w=a["ln_w"].reshape(D, 1),
        gate_b=np.broadcast_to(a["bg"].reshape(1, 1, E), (P, UT, E)),
        w0=a["W0"],
        w1=a["W1"],
        w2=a["W2"].reshape(E, HC, P, D).transpose(0, 2, 1, 3),
        b0=a["b0"].reshape(E * HC, P).T,
        b1=a["b1"].reshape(E * HC, P).T,
        b2=np.broadcast_to(a["b2"].reshape(1, E * D), (P, E * D)),
        ident_in=np.eye(P, dtype=f32),
        below_in=(row < col).astype(f32),
        heads_in=(row // HD == np.arange(H)[None, :]).astype(f32),
        spread_in=spread,
        collect_in=collect,
        center_in=np.eye(P, dtype=f32) - f32(1.0 / P),
        iota_in=np.broadcast_to(np.arange(TABLE)[None, :], (P, TABLE)).astype(f32),
        token_in=token.astype(f32),
        rank_in=np.broadcast_to((E - np.arange(E)).reshape(1, E, 1), (P, E, TILES)).astype(f32),
    )
    nc = bacc.Bacc("TRN2", target_bir_lowering=False, num_devices=1)
    args, given = {}, {}
    for name, array in arrays.items():
        given[f"in_{name}"] = np.ascontiguousarray(array)
        args[name] = nc.dram_tensor(f"in_{name}", array.shape, mybir.dt.from_np(array.dtype),
                                    kind="ExternalInput").ap()
    args["out"] = nc.dram_tensor("out_rows", (T, D), F32, kind="ExternalOutput").ap()
    build(nc, **args)
    got = run_bass_kernel_spmd(nc, [given], core_ids=[0]).results[0]["out_rows"]
    return got.reshape(T // SEQ, SEQ, D)
```

```python
from contextlib import ExitStack

import numpy as np

import concourse.bass as bass
from concourse import mybir

F32 = mybir.dt.float32
F32R = mybir.dt.float32r
BF16 = mybir.dt.bfloat16
I32 = mybir.dt.int32
U32 = mybir.dt.uint32
ALU = mybir.AluOpType
ACT = mybir.ActivationFunctionType
AX = mybir.AxisListType

P = 128
D = 128
H = 16
HD = D // H
SEQ = 256
T = 32 * SEQ
TILES = T // P
UNIT = 512
UNITS = T // UNIT
UT = UNIT // P
E = 8
HID = 512
HC = HID // P
BLOCK = 512
HALF = BLOCK // 2
SUBS = HALF // P
MAX_BLOCKS = 2 * T // BLOCK + E - 1
MIN_BLOCKS = 2 * T // BLOCK
TABLE = (MAX_BLOCKS + 1) * BLOCK // P
EPS = 1e-5
NORM_MIN_SQ = 1e-24
POOL_CONSTS = 6 + HD
KEYS_FIRST = 4
POOL_V = (0, 2, 4, 6)
DVE_V = tuple(v for v in range(HD) if v not in POOL_V)
Q, K, V, F, L, G = range(6)


def build(nc, x, w_proj, wg1, wg2t, wot, ln_w, gate_b, w0, w1, w2, b0, b1, b2,
          ident_in, below_in, heads_in, spread_in, collect_in, center_in, iota_in, token_in, rank_in, out):
    xn_dram = nc.dram_tensor("xn_dram", [T, D], F32, kind="Internal").ap()
    y_dram = nc.dram_tensor("y_dram", [MAX_BLOCKS * BLOCK, D], F32, kind="Internal").ap()
    x_units = x.rearrange("(u j p) d -> u p j d", p=P, j=UT)
    xn_units = xn_dram.rearrange("(u j p) d -> u p j d", p=P, j=UT)
    out_units = out.rearrange("(u j p) d -> u p j d", p=P, j=UT)
    y_halves = y_dram.rearrange("(n s p) d -> n p s d", p=P, s=SUBS)

    with ExitStack() as ctx:
        def sb(name, shape, dt=F32, to=ctx):
            return to.enter_context(nc.sbuf_tensor(name, shape, dt))

        def sem(name):
            return ctx.enter_context(nc.semaphore(name))

        psum = ctx.enter_context(nc.psum_tensor("psum", [P, 8, 512], F32))
        bank = [psum[:, i, :] for i in range(8)]
        logits_ps = [psum[:, 4 + i, 0:UT * E] for i in range(2)]
        g_ps, h_ps = ([psum[:, c, first:first + HALF] for c in range(HC)] for first in (0, HALF))
        proj_ps, turn_ps, wo_ps = bank[0], bank[5], bank[6]
        spread_ps = [bank[1 + v % 3] for v in range(HD)]
        o_ps = [bank[4], bank[7]]
        squares_ps = psum[:, 5:7, :].rearrange("p b n -> p (b n)")

        x_hi = sb("x_hi", [P, T], F32R)
        x_lo = sb("x_lo", [P, T], F32R)
        keys = sb("keys", [P, T])
        inv_norm = sb("inv_norm", [P, TILES * H])
        ident = sb("ident", [P, P])
        proj_hi = sb("proj_hi", [P, 6, D], F32R)
        proj_lo = sb("proj_lo", [P, 6, D], F32R)
        wo_c = sb("wo_c", [P, D])
        collect = sb("collect", [P, HD, P])
        spread = sb("spread", [P, HD, P], F32R)
        weight1 = sb("weight1", [P, TILES])
        weight2 = sb("weight2", [P, TILES])
        slots_u = sb("slots_u", [P, 2, TILES], U32)
        token_of = sb("token_of", [P, TABLE], U32)
        tokens_now = sb("tokens_now", [P, 2, SUBS], U32)
        slots_now = sb("slots_now", [P, 2, 2, UT], U32)
        starts = sb("starts", [P, E], I32)
        ends = sb("ends", [P, E], I32)
        k_len = sb("k_len", [P, TILES * H])
        eps_col = sb("eps_col", [P, 1])
        probe = sb("probe", [P, 1])

        early = ExitStack()
        x_rows = sb("x_rows", [P, 4, UT, D], to=early)
        xn_rows = sb("xn_rows", [P, 4, UT, D], to=early)
        spread_raw = sb("spread_raw", [P, HD, P], to=early)
        proj_raw = sb("proj_raw", [P, 5, D], to=early)
        wg1_s = sb("wg1_s", [HD, D], to=early)
        wg2t_s = sb("wg2t_s", [HD, D], to=early)
        wot_s = sb("wot_s", [P, D], to=early)
        wo_l = sb("wo_l", [P, D], to=early)
        lnw_s = sb("lnw_s", [P, 1], to=early)
        center = sb("center", [P, P], to=early)
        heads = sb("heads", [P, H], to=early)
        logits_t = sb("logits_t", [E, 2, UNIT], to=early)
        zeros = sb("zeros", [P, BLOCK // P, D], to=early)
        bn = sb("bn", [P, 4, UT, 6], to=early)
        mean_var = sb("mean_var", [P, 4, UT, 2], to=early)
        std = sb("std", [P, 4, UT], to=early)
        rstd = sb("rstd", [P, 4, UT], to=early)
        k_sq = sb("k_sq", [P, 2, UNIT], to=early)
        ss = sb("ss", [P, TILES * H], to=early)
        bias_g = sb("bias_g", [P, UT, E], to=early)
        rank_c = sb("rank_c", [P, E, TILES], to=early)
        logits = sb("logits", [P, E, TILES], to=early)
        logits2 = sb("logits2", [P, E, TILES], to=early)
        eq = sb("eq", [P, E, TILES], to=early)
        cand = sb("cand", [P, E, TILES], to=early)
        one1 = sb("one1", [P, E, TILES], to=early)
        one2 = sb("one2", [P, E, TILES], to=early)
        chosen = sb("chosen", [P, E, TILES], BF16, to=early)
        top1 = sb("top1", [P, TILES], to=early)
        top2 = sb("top2", [P, TILES], to=early)
        first1 = sb("first1", [P, TILES], to=early)
        first2 = sb("first2", [P, TILES], to=early)
        gap = sb("gap", [P, TILES], to=early)
        e_gap = sb("e_gap", [P, TILES], to=early)
        e_sum = sb("e_sum", [P, TILES], to=early)
        counts = sb("counts", [P, E, TILES], to=early)
        not_first = sb("not_first", [P, E, TILES], to=early)
        upto = sb("upto", [P, E, TILES], to=early)
        place_a = sb("place_a", [P, E, TILES], to=early)
        place_b = sb("place_b", [P, E, TILES], to=early)
        place = sb("place", [P, E, TILES], to=early)
        over = sb("over", [P, E, T // BLOCK], to=early)
        blocks_of = sb("blocks_of", [P, E], to=early)
        blocks_min = sb("blocks_min", [P, E], to=early)
        ones_e = sb("ones_e", [P, E], to=early)
        end_f = sb("end_f", [P, E], to=early)
        start_f = sb("start_f", [P, E], to=early)
        picked = sb("picked", [P, E, TILES], to=early)
        slots_f = sb("slots_f", [P, 2, TILES], to=early)
        row_u = sb("row_u", [P, 2, TILES], U32, to=early)
        tile_u = sb("tile_u", [P, 2, TILES], U32, to=early)
        row_f = sb("row_f", [P, 2, TILES], to=early)
        tile_f = sb("tile_f", [P, 2, TILES], to=early)
        iota = sb("iota", [P, TABLE], to=early)
        token_c = sb("token_c", [P, TILES], to=early)
        below_raw = sb("below_raw", [P, P], to=early)
        below = sb("below", [P, P], BF16, to=early)
        ones_b = sb("ones_b", [P, P], BF16, to=early)
        zero_r = sb("zero_r", [P, TABLE], F32R, to=early)
        is_row = sb("is_row", [P, 2 * UT, P], F32R, to=early)
        is_tile = sb("is_tile", [P, 2 * UT, TABLE], F32R, to=early)
        early.close()

        mid = ExitStack()
        w_raw = sb("w_raw", [P, 2, 2, HID], to=mid)
        w2_s = sb("w2_s", [P, 2, HC, D], to=mid)
        slot_rows = sb("slot_rows", [P, 2, SUBS, D], to=mid)
        b0_s = sb("b0_s", [P, E * HC], to=mid)
        b1_s = sb("b1_s", [P, E * HC], to=mid)
        b2_s = sb("b2_s", [P, E * D], to=mid)
        xs_hi = sb("xs_hi", [P, 2, HALF], F32R, to=mid)
        xs_lo = sb("xs_lo", [P, 2, HALF], F32R, to=mid)
        w_hi = sb("w_hi", [P, 2, 2, HID], F32R, to=mid)
        w_lo = sb("w_lo", [P, 2, 2, HID], F32R, to=mid)
        gated = sb("gated", [P, HC, HALF], to=mid)
        hidden = sb("hidden", [P, 2, HC, HALF], to=mid)
        y_rows = sb("y_rows", [P, 2, SUBS, D], to=mid)
        mid.close()

        late = ExitStack()
        q_s = sb("q_s", [P, 2, UNIT], to=late)
        v_s = sb("v_s", [P, 2, UNIT], to=late)
        v_hi = sb("v_hi", [P, 2, UNIT], F32R, to=late)
        v_lo = sb("v_lo", [P, 2, UNIT], F32R, to=late)
        decay_t = sb("decay_t", [P, UNIT], to=late)
        decay = sb("decay", [P, 2, UNIT], to=late)
        gate_t = sb("gate_t", [P, 2, UNIT], to=late)
        k_n = sb("k_n", [P, 2, UNIT], to=late)
        kv = sb("kv", [P, 2, UNIT], to=late)
        state = sb("state", [P, 4, UNIT], to=late)
        q_state = sb("q_state", [P, 4, UNIT], to=late)
        o_s = sb("o_s", [P, 2, UNIT], to=late)
        bn_o = sb("bn_o", [P, UT, 6], to=late)
        mv_o = sb("mv_o", [P, 2, UT, 2], to=late)
        std_o = sb("std_o", [P, 2, UT], to=late)
        rstd_o = sb("rstd_o", [P, 2, UT], to=late)
        x_res = sb("x_res", [P, 2, UT, D], to=late)
        y1 = sb("y1", [P, 2, UT, D], to=late)
        y2 = sb("y2", [P, 2, UT, D], to=late)
        y12 = sb("y12", [P, 2, UT, D], to=late)
        attn_x = sb("attn_x", [P, 2, UT, D], to=late)
        out_s = sb("out_s", [P, 2, UT, D], to=late)
        inv_u = sb("inv_u", [P, 2, UT * H, HD], to=late)
        late.close()

        consts_in = sem("consts_in")
        stood = sem("stood")
        early_consts = sem("early_consts")
        proj_in = sem("proj_in")
        pool_consts = sem("pool_consts")
        x_in = [sem(f"x_in{m}") for m in range(4)]
        bn_ready = sem("bn_ready")
        stats_ready = sem("stats_ready")
        std_ready = sem("std_ready")
        rstd_ready = sem("rstd_ready")
        xn_ready = sem("xn_ready")
        xn_out = [sem(f"xn_out{m}") for m in range(4)]
        turned = sem("turned")
        hi_ready = sem("hi_ready")
        lo_ready = sem("lo_ready")
        logits_t_done = sem("logits_t_done")
        logits_t_ready = sem("logits_t_ready")
        logits_done = sem("logits_done")
        logits_ready = sem("logits_ready")
        zeros_ready = sem("zeros_ready")
        zeros_out = sem("zeros_out")
        rows_stored = sem("rows_stored")
        fold_ps = sem("fold_ps")
        fold = sem("fold")
        g_hi_ready = sem("g_hi_ready")
        folded = sem("folded")
        k_done = sem("k_done")
        k_ready = sem("k_ready")
        sq_ready = sem("sq_ready")
        ss_done = sem("ss_done")
        ss_ready = sem("ss_ready")
        len_ready = sem("len_ready")
        route = sem("route")
        gap_ready = sem("gap_ready")
        gap_exp = sem("gap_exp")
        chosen_ready = sem("chosen_ready")
        counts_done = sem("counts_done")
        onehot_ready = sem("onehot_ready")
        onehot_used = sem("onehot_used")
        table_done = sem("table_done")
        routed = sem("routed")
        raw_in = [sem("raw_in0"), sem("raw_in1")]
        w2_in = [sem("w2_in0"), sem("w2_in1")]
        bias_in = sem("bias_in")
        w_hi_ready = sem("w_hi_ready")
        w_split = sem("w_split")
        inv_ready = sem("inv_ready")
        rows_in = [sem("rows_in0"), sem("rows_in1")]
        xs_turned = sem("xs_turned")
        tokens_ready = sem("tokens_ready")
        slots_ready = sem("slots_ready")
        xs_hi_ready = sem("xs_hi_ready")
        xs_ready = sem("xs_ready")
        up_done = sem("up_done")
        gated_ready = sem("gated_ready")
        hidden_ready = sem("hidden_ready")
        down_done = sem("down_done")
        y_ready = sem("y_ready")
        y_out = [sem("y_out0"), sem("y_out1")]
        experts_over = sem("experts_over")
        proj_done = sem("proj_done")
        proj_read = sem("proj_read")
        v_hi_ready = sem("v_hi_ready")
        v_lo_ready = sem("v_lo_ready")
        decay_ready = sem("decay_ready")
        decay_reset = sem("decay_reset")
        inv_ready_u = sem("inv_ready_u")
        inv_turned = sem("inv_turned")
        kn_ready = sem("kn_ready")
        spread_done = sem("spread_done")
        kv_ready = sem("kv_ready")
        state_ready = sem("state_ready")
        qs_pool = sem("qs_pool")
        qs_dve = sem("qs_dve")
        collected = sem("collected")
        o_ready = sem("o_ready")
        o_turned = sem("o_turned")
        out_done = sem("out_done")
        bn_o_ready = sem("bn_o_ready")
        var_ready = sem("var_ready")
        std_o_ready = sem("std_o_ready")
        rstd_o_ready = sem("rstd_o_ready")
        res_in = [sem("res_in0"), sem("res_in1")]
        y_in = [sem("y_in0"), sem("y_in1")]
        y_scaled = sem("y_scaled")
        y12_ready = sem("y12_ready")
        attn_x_ready = sem("attn_x_ready")
        sum_ready = sem("sum_ready")
        out_out = [sem("out_out0"), sem("out_out1")]


        FIRST_LOADS = [(ident, ident_in), (proj_raw, w_proj)]
        EARLY_LOADS = [(wg1_s, wg1), (wg2t_s, wg2t),
                       (wot_s, wot), (lnw_s, ln_w), (center, center_in), (heads, heads_in),
                       (spread_raw, spread_in), (collect, collect_in), (bias_g, gate_b), (rank_c, rank_in),
                       (iota, iota_in), (token_c, token_in), (below_raw, below_in)]

        def wait(eng, semaphore, value):
            if not (isinstance(value, int) and value <= 0):
                eng.wait_ge(semaphore, value)

        def stand_apart(eng):
            eng.sem_inc(stood, 1)

        def units_in_pairs(eng, body):
            for u in range(4):
                body(u, u % 2, u // 2)
            with eng.Fori(2, UNITS // 2) as i:
                body(2 * i, 0, i)
                body(2 * i + 1, 1, i)

        def pipeline(eng, body):
            for u in range(4):
                body(u, u, 0)
            with eng.Fori(1, UNITS // 4) as i:
                for m in range(4):
                    body(4 * i + m, m, i)
            for u in range(UNITS, UNITS + 4):
                body(u, u % 4, u // 4)

        def back(u, m, k, n):
            return u - n, (m - n) % 4, k + (m - n) // 4

        def exists(u):
            return not isinstance(u, int) or 0 <= u < UNITS

        def units_in_steps(eng, step):
            for u in range(5):
                step(u, u % 2, u // 2, u == 0, False)
            with eng.Fori(2, UNITS // 2 - 1) as i:
                step(2 * i + 1, 1, i, False, False)
                step(2 * i + 2, 0, i + 1, False, False)
            step(UNITS - 1, 1, UNITS // 2 - 1, False, True)

        def block_range(eng, e):
            start = eng.value_load(starts[0:1, bass.ds(e, 1)], min_val=0, max_val=MAX_BLOCKS)
            end = eng.value_load(ends[0:1, bass.ds(e, 1)], min_val=1, max_val=MAX_BLOCKS)
            return start, end

        def all_blocks(eng):
            return eng.value_load(ends[0:1, E - 1:E], min_val=1, max_val=MAX_BLOCKS)

        def one(view, i):
            if isinstance(i, int):
                return view[i]
            if len(view.shape) == 4:
                return view[bass.ds(i, 1)].rearrange("u p j d -> (u p) j d")
            return view[bass.ds(i, 1)].rearrange("u p d -> (u p) d")

        block = ctx.enter_context(nc.Block())

        @block.sync
        def _(sp):
            def load_x(u, m):
                sp.dma_start(x_rows[:, m], one(x_units, u)).then_inc(x_in[m], 16)

            load_x(0, 0)
            for dst, src in FIRST_LOADS:
                sp.dma_start(dst[:], src).then_inc(proj_in, 16)
            for u in range(1, 4):
                load_x(u, u)
            for dst, src in EARLY_LOADS:
                sp.dma_start(dst[:], src).then_inc(consts_in, 16)

            sp.wait_ge(zeros_ready, 1)
            for b in range(MIN_BLOCKS, MAX_BLOCKS):
                sp.dma_start(y_dram[BLOCK * b:BLOCK * b + BLOCK].rearrange("(j p) d -> p j d", p=P), zeros[:]
                             ).then_inc(zeros_out, 16)

            def store_rows(u, m):
                sp.wait_ge(xn_ready, u + 1)
                sp.dma_start(one(xn_units, u), xn_rows[:, m]).then_inc(xn_out[m], 16)

            with sp.Fori(0, UNITS // 4 - 1) as i:
                for m in range(4):
                    store_rows(4 * i + m, m)
                    load_x(4 * i + m + 4, m)
            for m in range(4):
                store_rows(UNITS - 4 + m, m)
            for m in range(4):
                sp.wait_ge(xn_out[m], 16 * (UNITS // 4))
            sp.wait_ge(zeros_out, 16 * (MAX_BLOCKS - MIN_BLOCKS))
            sp.sem_inc(rows_stored, 1)

            def load_raw(e, par):
                sp.dma_start(w_raw[:, par, 0], one(w0, e)).then_inc(raw_in[par], 16)
                sp.dma_start(w_raw[:, par, 1], one(w1, e)).then_inc(raw_in[par], 16)

            def load_w2(e, par):
                sp.dma_start(w2_s[:, par], one(w2, e)).then_inc(w2_in[par], 16)

            sp.wait_ge(turned, UNITS)
            sp.wait_ge(fold, 3)
            sp.wait_ge(folded, 2)
            sp.wait_ge(pool_consts, POOL_CONSTS)
            load_raw(0, 0)
            load_w2(0, 0)
            for dst, src in ((b0_s, b0), (b1_s, b1), (b2_s, b2)):
                sp.dma_start(dst[:], src).then_inc(bias_in, 16)
            load_raw(1, 1)
            sp.wait_ge(routed, 1)
            for h in range(2):
                sp.sem_inc(y_out[h], 16)
            with sp.Fori(0, E // 2) as pair:
                for ep in range(2):
                    e = 2 * pair + ep
                    start, end = block_range(sp, e)
                    sp.wait_ge(down_done, 2 * start + 2)
                    load_w2((e + 1) % E, 1 - ep)
                    sp.wait_ge(w_split, e + 1)
                    load_raw((e + 2) % E, ep)
                    with sp.Fori(start, end) as b:
                        for h in range(2):
                            sp.wait_ge(y_ready, 2 * b + h + 3)
                            sp.dma_start(one(y_halves, 2 * b + h), y_rows[:, h]).then_inc(y_out[h], 16)
            total = all_blocks(sp)
            for h in range(2):
                sp.wait_ge(y_out[h], 16 * total + 16)
                sp.wait_ge(raw_in[h], 32 * (E // 2 + 1))
                sp.wait_ge(rows_in[h], 32 * total + 32)
            sp.wait_ge(w2_in[0], 16 * (E // 2 + 1))
            sp.wait_ge(w_split, E + 1)
            sp.wait_ge(xs_ready, 2 * total + 2)
            sp.sem_inc(experts_over, 1)

            def load_res(u, par):
                wait(sp, attn_x_ready, u - 1)
                sp.dma_start(x_res[:, par], one(x_units, u)).then_inc(res_in[par], 16)

            def store(u, par):
                sp.wait_ge(sum_ready, u + 1)
                sp.dma_start(one(out_units, u), out_s[:, par]).then_inc(out_out[par], 16)

            load_res(0, 0)
            load_res(1, 1)
            with sp.Fori(0, UNITS // 2 - 1) as i:
                for par in range(2):
                    store(2 * i + par, par)
                    load_res(2 * i + par + 2, par)
            store(UNITS - 2, 0)
            store(UNITS - 1, 1)
            for par in range(2):
                sp.wait_ge(out_out[par], 16 * (UNITS // 2))

        @block.gpsimd
        def _(pool):
            pool.memset(zeros[:], 0.0).then_inc(zeros_ready, 1)
            pool.memset(ones_b[:], 1.0).then_inc(pool_consts, 1)
            pool.memset(ones_e[:], 1.0).then_inc(pool_consts, 1)
            pool.memset(not_first[:, :, 1:TILES], 1.0).then_inc(pool_consts, 1)
            pool.memset(not_first[:, :, 0:1], 0.0).then_inc(pool_consts, 1)
            pool.wait_ge(zeros_ready, 1)
            pool.tensor_copy(zero_r[:], zeros[:].rearrange("p j d -> p (j d)")[:, 0:TABLE]).then_inc(pool_consts, 1)
            pool.wait_ge(consts_in, 16 * len(EARLY_LOADS))
            pool.tensor_copy(below[:], below_raw[:]).then_inc(pool_consts, 1)
            for v in range(HD):
                pool.tensor_copy(spread[:, v], spread_raw[:, v]).then_inc(pool_consts, 1)

            pool.wait_ge(routed, 1)
            pool.wait_ge(turned, UNITS)
            pool.wait_ge(rows_stored, 1)
            total = all_blocks(pool)
            with pool.Fori(0, total + 1) as b:
                for h in range(2):
                    pool.wait_ge(xs_turned, 2 * b + h + 1)
                    at = bass.ds((2 * b + h) * SUBS, SUBS)
                    pool.tensor_copy(tokens_now[:, h], token_of[:, at]).then_inc(tokens_ready, 1)
                    pool.wait_ge(tokens_ready, 2 * b + h + 1)
                    stand_apart(pool)
                    for s in range(SUBS):
                        pool.indirect_dma_start(slot_rows[:, h, s], None, xn_dram,
                                                bass.IndirectOffsetOnAxis(tokens_now[:, h, s:s + 1], 0)
                                                ).then_inc(rows_in[h], 16)

            pool.wait_ge(experts_over, 1)

            def add_rows(u, par):
                pool.wait_ge(y_scaled, u + 1)
                wait(pool, sum_ready, u - 1)
                pool.tensor_tensor(y12[:, par], y1[:, par], y2[:, par], ALU.add).then_inc(y12_ready, 1)

            def step(u, par, k, first, last):
                wait(pool, y12_ready, u - 1)
                pool.tensor_copy(slots_now[:, par], slots_u[:, :, bass.ds(UT * u, UT)]).then_inc(slots_ready, 1)
                pool.wait_ge(slots_ready, u + 1)
                for n, v in enumerate(POOL_V):
                    pool.wait_ge(state_ready, HD * u + v + 1)
                    wait(pool, collected, HD * u + v - 3)
                    pool.tensor_tensor(q_state[:, v % 4], state[:, v % 4], q_s[:, par], ALU.mult
                                       ).then_inc(qs_pool, 1)
                    for choice, rows in ((0, y1), (1, y2)):
                        pool.indirect_dma_start(
                            rows[:, par, n], None, y_dram,
                            bass.IndirectOffsetOnAxis(slots_now[:, par, choice, n:n + 1], 0),
                        ).then_inc(y_in[par], 16)
                    if n == 1 and not first:
                        add_rows(u - 1, 1 - par)

            assert len(POOL_V) == UT
            units_in_steps(pool, step)
            add_rows(UNITS - 1, 1)

        @block.scalar
        def _(act):
            act.wait_ge(early_consts, 1)

            def std_of(u, m):
                act.wait_ge(stats_ready, u + 1)
                wait(act, rstd_ready, u - 3)
                act.activation(std[:, m], mean_var[:, m, :, 1], ACT.Sqrt, bias=eps_col[:, 0:1]
                               ).then_inc(std_ready, 1)

            def high_part(u, par):
                act.wait_ge(turned, u + 1)
                stand_apart(act)
                act.activation(x_hi[:, bass.ds(UNIT * u, UNIT)], bank[par][:, :], ACT.Copy).then_inc(hi_ready, 1)

            def logits_row(u, par):
                act.wait_ge(logits_t_done, u + 1)
                wait(act, logits_done, u - 1)
                act.activation(logits_t[:, par], bank[2 + par][0:E, :], ACT.Copy).then_inc(logits_t_ready, 1)

            def step_1(u, m, k):
                if exists(u):
                    std_of(u, m)
                if exists(u - 1):
                    high_part(u - 1, (m - 1) % 2)
                if exists(u - 2):
                    logits_row(u - 2, m % 2)

            pipeline(act, step_1)

            def key_unit(u, par, k):
                act.wait_ge(k_done, u + 1)
                stand_apart(act)
                act.activation(keys[:, bass.ds(UNIT * u, UNIT)], bank[2 + par][:, :], ACT.Silu).then_inc(k_ready, 1)
                act.wait_ge(k_ready, u + 1)
                wait(act, ss_done, u - 1)
                stand_apart(act)
                act.activation(k_sq[:, par], keys[:, bass.ds(UNIT * u, UNIT)], ACT.Square).then_inc(sq_ready, 1)

            for u in range(KEYS_FIRST):
                key_unit(u, u % 2, u // 2)
            act.wait_ge(gap_ready, 1)
            act.activation(e_gap[:], gap[:], ACT.Exp).then_inc(gap_exp, 1)
            with act.Fori(KEYS_FIRST // 2, UNITS // 2) as i:
                key_unit(2 * i, 0, i)
                key_unit(2 * i + 1, 1, i)
            act.wait_ge(ss_ready, 2)
            act.activation(k_len[:], ss[:], ACT.Sqrt).then_inc(len_ready, 1)

            def load_silu_table():
                act.activation(probe[:, 0:1], eps_col[:, 0:1], ACT.Silu)

            act.wait_ge(routed, 1)
            act.wait_ge(bias_in, 48)

            def xs_high_part(n, h):
                act.wait_ge(xs_turned, n + 3)
                act.activation(xs_hi[:, h], bank[6 + h][:, 0:HALF], ACT.Copy).then_inc(xs_hi_ready, 1)

            def weights_high_part(s, par, k):
                act.wait_ge(raw_in[par], 32 * (k + 1))
                for i in range(2):
                    act.activation(w_hi[:, par, i], w_raw[:, par, i], ACT.Copy).then_inc(w_hi_ready, 1)

            weights_high_part(0, 0, 0)
            for h in range(2):
                xs_high_part(h, h)
            with act.Fori(0, E // 2) as pair:
                for ep in range(2):
                    e = 2 * pair + ep
                    start, end = block_range(act, e)
                    act.wait_ge(down_done, 2 * start + 2)
                    weights_high_part(e + 1, 1 - ep, pair + ep)
                    with act.Fori(start, end) as b:
                        load_silu_table()
                        for h in range(2):
                            for c in range(HC):
                                n = (2 * b + h) * HC + c
                                act.wait_ge(up_done, n + 1)
                                act.wait_ge(hidden_ready, n + 1)
                                stand_apart(act)
                                act.activation(gated[:, c], g_ps[c], ACT.Silu,
                                               bias=b1_s[:, bass.ds(HC * e + c, 1)]).then_inc(gated_ready, 1)
                        for h in range(2):
                            xs_high_part(2 * b + 2 + h, h)

            act.wait_ge(experts_over, 1)

            def head(u, par):
                wait(act, o_ready, u - 1)
                stand_apart(act)
                act.activation(inv_u[:, par], inv_norm[:, bass.ds(UT * H * u, UT * H)].unsqueeze(2)
                               .broadcast_to([P, UT * H, HD]), ACT.Copy).then_inc(inv_ready_u, 1)
                act.wait_ge(proj_done, 4 * u + 1)
                act.activation(v_s[:, par], proj_ps, ACT.Silu).then_inc(proj_read, 1)
                act.wait_ge(proj_read, 4 * u + 1)
                act.activation(v_hi[:, par], v_s[:, par], ACT.Copy).then_inc(v_hi_ready, 1)
                act.wait_ge(proj_done, 4 * u + 2)
                act.activation(q_s[:, par], proj_ps, ACT.Silu).then_inc(proj_read, 1)
                act.wait_ge(proj_done, 4 * u + 3)
                wait(act, decay_ready, u)
                act.activation(decay_t[:], proj_ps, ACT.Tanh, scale=0.5).then_inc(proj_read, 1)
                act.wait_ge(proj_done, 4 * u + 4)
                act.activation(gate_t[:, par], proj_ps, ACT.Tanh, scale=0.5).then_inc(proj_read, 1)
                act.wait_ge(proj_read, 4 * u + 3)
                act.activation(decay[:, par], decay_t[:], ACT.Copy, scale=0.5, bias=0.5).then_inc(decay_ready, 1)

            def weight_rows(u, par, k):
                act.wait_ge(y_in[par], 16 * 2 * UT * (k + 1))
                stand_apart(act)
                for j in range(UT):
                    for rows, weight in ((y1, weight1), (y2, weight2)):
                        ins = act.activation(rows[:, par, j], rows[:, par, j], ACT.Copy,
                                             scale=weight[:, bass.ds(UT * u + j, 1)])
                ins.then_inc(y_scaled, 1)

            def std_of_o(u, par):
                act.wait_ge(var_ready, u + 1)
                wait(act, rstd_o_ready, u - 1)
                act.activation(std_o[:, par], mv_o[:, par, :, 1], ACT.Sqrt, bias=eps_col[:, 0:1]
                               ).then_inc(std_o_ready, 1)

            def step(u, par, k, first, last):
                if not last:
                    load_silu_table()
                if not first:
                    weight_rows(u - 1, 1 - par, k if par else k - 1)
                if not last:
                    head(u + 1, 1 - par)
                if not first:
                    std_of_o(u - 1, 1 - par)

            head(0, 0)
            units_in_steps(act, step)
            weight_rows(UNITS - 1, 1, UNITS // 2 - 1)
            std_of_o(UNITS - 1, 1)

        @block.vector
        def _(dve):
            sub, mul, add = ALU.subtract, ALU.mult, ALU.add
            dve.memset(eps_col[:], EPS).then_inc(early_consts, 1)
            dve.sem_inc(logits_ready, 2)
            dve.wait_ge(proj_in, 16 * len(FIRST_LOADS))
            dve.tensor_copy(proj_hi[:, 0:G], proj_raw[:]).then_inc(fold, 1)
            dve.wait_ge(fold, 1)
            dve.tensor_tensor(proj_lo[:, 0:G], proj_raw[:], proj_hi[:, 0:G].bitcast(F32), sub).then_inc(fold, 1)

            def statistics(u, m, k):
                dve.wait_ge(x_in[m], 16 * (k + 1))
                wait(dve, xn_ready, u - 3)
                for j in range(UT):
                    ins = dve.bn_stats(bn[:, m, j], x_rows[:, m, j])
                ins.then_inc(bn_ready, 1)

            def means(u, m):
                dve.wait_ge(bn_ready, u + 1)
                stand_apart(dve)
                for j in range(UT):
                    ins = dve.bn_aggr(mean_var[:, m, j], bn[:, m, j])
                ins.then_inc(stats_ready, 1)

            def inverse_std(u, m):
                dve.wait_ge(std_ready, u + 1)
                dve.reciprocal(rstd[:, m], std[:, m]).then_inc(rstd_ready, 1)

            def norm_rows(u, m, k):
                dve.wait_ge(rstd_ready, u + 1)
                wait(dve, turned, u - 3)
                wait(dve, xn_out[m], 16 * k)
                for j in range(UT):
                    ins = dve.tensor_scalar(xn_rows[:, m, j], x_rows[:, m, j], mean_var[:, m, j, 0:1],
                                            rstd[:, m, j:j + 1], sub, mul)
                ins.then_inc(xn_ready, 1)

            def low_part(u, par):
                at = bass.ds(UNIT * u, UNIT)
                dve.wait_ge(hi_ready, u + 1)
                dve.tensor_tensor(x_lo[:, at], bank[par][:, :], x_hi[:, at].bitcast(F32), sub).then_inc(lo_ready, 1)

            def take_logits(u, par):
                dve.wait_ge(logits_done, u + 1)
                dve.tensor_tensor(logits[:, :, bass.ds(UT * u, UT)].rearrange("p e j -> p j e"),
                                  logits_ps[par].rearrange("p (j e) -> p j e", e=E), bias_g[:], add
                                  ).then_inc(logits_ready, 1)

            def step_1(u, m, k):
                if exists(u):
                    statistics(u, m, k)
                if exists(u - 1):
                    inverse_std(u - 1, (m - 1) % 4)
                if exists(u):
                    means(u, m)
                if exists(u - 1):
                    norm_rows(*back(u, m, k, 1))
                if exists(u - 2):
                    low_part(u - 2, m % 2)
                if isinstance(u, int) and u == 3:
                    fold_weights()
                if exists(u - 4):
                    take_logits(u - 4, m % 2)

            def fold_weights():
                dve.wait_ge(consts_in, 16 * len(EARLY_LOADS))
                dve.tensor_scalar(wo_l[:], wot_s[:], lnw_s[:, 0:1], None, mul).then_inc(fold, 1)
                dve.wait_ge(fold_ps, 2)
                dve.tensor_copy(proj_hi[:, G], bank[7][:, 0:D]).then_inc(g_hi_ready, 1)
                dve.wait_ge(g_hi_ready, 1)
                dve.tensor_tensor(proj_lo[:, G], bank[7][:, 0:D], proj_hi[:, G].bitcast(F32), sub).then_inc(folded, 1)
                dve.tensor_copy(wo_c[:], bank[7][:, D:2 * D]).then_inc(folded, 1)

            pipeline(dve, step_1)

            n_route = [0]

            def step_done(ins):
                n_route[0] += 1
                ins.then_inc(route, 1)
                dve.wait_ge(route, n_route[0])

            def over_experts(a):
                return a.unsqueeze(1).broadcast_to([P, E, TILES])

            dve.wait_ge(pool_consts, POOL_CONSTS)
            dve.wait_ge(logits_ready, UNITS + 2)
            source = logits
            for top, first_e, pick in ((top1, first1, one1), (top2, first2, one2)):
                step_done(dve.tensor_reduce(top[:], source[:].rearrange("p e t -> p t e"), AX.X, ALU.max))
                if source is logits2:
                    step_done(dve.tensor_tensor(gap[:], top2[:], top1[:], sub))
                    dve.sem_inc(gap_ready, 1)
                step_done(dve.tensor_tensor(eq[:], source[:], over_experts(top[:]), ALU.is_equal))
                step_done(dve.tensor_tensor(cand[:], eq[:], rank_c[:], mul))
                step_done(dve.tensor_reduce(first_e[:], cand[:].rearrange("p e t -> p t e"), AX.X, ALU.max))
                step_done(dve.tensor_tensor(pick[:], cand[:], over_experts(first_e[:]), ALU.is_equal))
                if source is logits:
                    step_done(dve.scalar_tensor_tensor(out=logits2[:], in0=pick[:], scalar=-3e38, in1=logits[:],
                                                       op0=mul, op1=add))
                    source = logits2
            dve.tensor_tensor(chosen[:], one1[:], one2[:], add).then_inc(chosen_ready, 1)
            dve.wait_ge(gap_exp, 1)
            step_done(dve.tensor_scalar(e_sum[:], e_gap[:], 1.0, None, add))
            step_done(dve.reciprocal(weight1[:], e_sum[:]))
            step_done(dve.tensor_tensor(weight2[:], e_gap[:], weight1[:], mul))
            dve.wait_ge(counts_done, 1)
            step_done(dve.tensor_copy(counts[:].rearrange("p e t -> p (e t)"), bank[1][:, :]))
            step_done(dve.tensor_tensor_scan(upto[:].rearrange("p e t -> p (e t)"),
                                             not_first[:].rearrange("p e t -> p (e t)"),
                                             counts[:].rearrange("p e t -> p (e t)"), 0.0, mul, add))
            step_done(dve.scalar_tensor_tensor(
                out=over[:], in0=upto[:, :, TILES - 1:TILES].broadcast_to([P, E, T // BLOCK]), scalar=1.0 / BLOCK,
                in1=iota[:, 0:T // BLOCK].unsqueeze(1).broadcast_to([P, E, T // BLOCK]), op0=mul, op1=ALU.is_gt))
            step_done(dve.tensor_reduce(blocks_of[:], over[:], AX.X, add))
            step_done(dve.tensor_scalar(blocks_min[:], blocks_of[:], 1.0, None, ALU.max))
            step_done(dve.tensor_tensor_scan(end_f[:], ones_e[:], blocks_min[:], 0.0, mul, add))
            step_done(dve.tensor_tensor(start_f[:], end_f[:], blocks_min[:], sub))
            step_done(dve.tensor_copy(ends[:], end_f[:]))
            step_done(dve.tensor_copy(starts[:], start_f[:]))
            step_done(dve.tensor_tensor(place_a[:], upto[:], counts[:], sub))
            step_done(dve.tensor_tensor(place_b[:].rearrange("p e t -> p (e t)"), bank[0][:, :],
                                        place_a[:].rearrange("p e t -> p (e t)"), add))
            step_done(dve.scalar_tensor_tensor(out=place[:], in0=start_f[:].unsqueeze(2).broadcast_to([P, E, TILES]),
                                               scalar=float(BLOCK), in1=place_b[:], op0=mul, op1=add))
            for choice, pick in ((0, one1), (1, one2)):
                step_done(dve.tensor_tensor(picked[:], pick[:], place[:], mul))
                step_done(dve.tensor_reduce(slots_f[:, choice], picked[:].rearrange("p e t -> p t e"), AX.X, add))
            step_done(dve.tensor_copy(slots_u[:], slots_f[:]))
            step_done(dve.tensor_scalar(row_u[:], slots_u[:], P - 1, None, ALU.bitwise_and))
            step_done(dve.tensor_scalar(tile_u[:], slots_u[:], 7, None, ALU.logical_shift_right))
            step_done(dve.tensor_copy(row_f[:], row_u[:]))
            step_done(dve.tensor_copy(tile_f[:], tile_u[:]))

            def one_hots(u, par, k):
                for m in range(2 * UT):
                    j, choice = m // 2, m % 2
                    t = UT * u + j
                    row, tile = (a[:, choice, bass.ds(t, 1)] for a in (row_f, tile_f))
                    wait(dve, onehot_used, 2 * UT * (u - 1) + m + 1)
                    dve.tensor_scalar(is_row[:, m], iota[:, 0:P], row, None, ALU.is_equal).then_inc(onehot_ready, 1)
                    dve.tensor_scalar(is_tile[:, m], iota[:], tile, token_c[:, bass.ds(t, 1)],
                                      ALU.is_equal, mul).then_inc(onehot_ready, 1)

            units_in_pairs(dve, one_hots)
            dve.wait_ge(ss_done, UNITS)
            for i in range(2):
                dve.tensor_scalar(ss[:, 512 * i:512 * i + 512], bank[5 + i][:, :], NORM_MIN_SQ, None, ALU.max
                                  ).then_inc(ss_ready, 1)
            dve.wait_ge(table_done, 1)
            dve.tensor_scalar(token_of[:], bank[7][:, 0:TABLE], float(T // 2), None, add).then_inc(routed, 1)

            dve.wait_ge(routed, 1)
            dve.wait_ge(len_ready, 1)
            dve.wait_ge(bias_in, 48)
            dve.sem_inc(hidden_ready, HC)
            dve.sem_inc(y_ready, 2)

            def split_weights(s, par):
                for i in range(2):
                    dve.wait_ge(w_hi_ready, 2 * s + i + 1)
                    ins = dve.tensor_tensor(w_lo[:, par, i], w_raw[:, par, i], w_hi[:, par, i].bitcast(F32), sub)
                ins.then_inc(w_split, 1)

            def xs_low_part(n, h):
                dve.wait_ge(xs_hi_ready, n + 1)
                dve.tensor_tensor(xs_lo[:, h], bank[6 + h][:, 0:HALF], xs_hi[:, h].bitcast(F32), sub
                                  ).then_inc(xs_ready, 1)

            split_weights(0, 0)
            for h in range(2):
                xs_low_part(h, h)
            with dve.Fori(0, E // 2) as pair:
                for ep in range(2):
                    e = 2 * pair + ep
                    start, end = block_range(dve, e)
                    share = bass.ds(TILES * H // E * e, TILES * H // E)
                    dve.reciprocal(inv_norm[:, share], k_len[:, share]).then_inc(inv_ready, 1)
                    dve.wait_ge(down_done, 2 * start + 2)
                    split_weights(e + 1, 1 - ep)
                    with dve.Fori(start, end) as b:
                        for h in range(2):
                            dve.wait_ge(down_done, 2 * b + h + 1)
                            for c in range(HC):
                                n = (2 * b + h) * HC + c
                                dve.wait_ge(gated_ready, n + 1)
                                dve.scalar_tensor_tensor(out=hidden[:, h, c], in0=h_ps[c],
                                                         scalar=b0_s[:, bass.ds(HC * e + c, 1)],
                                                         in1=gated[:, c], op0=add, op1=mul
                                                         ).then_inc(hidden_ready, 1)
                        for h in range(2):
                            n = 2 * b + h
                            xs_low_part(n + 2, h)
                            dve.wait_ge(down_done, n + 3)
                            dve.wait_ge(y_out[h], 16 * b + 16)
                            for s in range(SUBS):
                                ins = dve.tensor_tensor(y_rows[:, h, s], bank[4 + h][:, D * s:D * s + D],
                                                        b2_s[:, bass.ds(D * e, D)], add)
                            ins.then_inc(y_ready, 1)

            dve.wait_ge(experts_over, 1)

            def low_v(u, par):
                wait(dve, o_ready, u - 1)
                dve.wait_ge(v_hi_ready, u + 1)
                dve.tensor_tensor(v_lo[:, par], v_s[:, par], v_hi[:, par].bitcast(F32), sub).then_inc(v_lo_ready, 1)

            def reset_decay(u, par):
                dve.wait_ge(decay_ready, u + 1)
                for s in range(UNIT // SEQ):
                    dve.memset(decay[:, par, SEQ * s:SEQ * s + 1], 0.0).then_inc(decay_reset, 1)

            def norm_keys(u, par):
                dve.wait_ge(inv_turned, u + 1)
                dve.tensor_tensor(k_n[:, par], turn_ps, keys[:, bass.ds(UNIT * u, UNIT)], mul
                                  ).then_inc(kn_ready, 1)

            def statistics_o(u, par):
                dve.wait_ge(o_turned, u + 1)
                wait(dve, std_o_ready, u - 1)
                wait(dve, var_ready, u)
                for j in range(UT):
                    ins = dve.bn_stats(bn_o[:, j], turn_ps[:, D * j:D * j + D])
                ins.then_inc(bn_o_ready, 1)

            def means_o(u, par):
                dve.wait_ge(bn_o_ready, u + 1)
                stand_apart(dve)
                for j in range(UT):
                    ins = dve.bn_aggr(mv_o[:, par, j], bn_o[:, j])
                ins.then_inc(var_ready, 1)

            def sum_up(u, par, k):
                dve.wait_ge(rstd_o_ready, u + 1)
                dve.wait_ge(out_done, u + 1)
                dve.wait_ge(res_in[par], 16 * (k + 1))
                for j in range(UT):
                    ins = dve.scalar_tensor_tensor(out=attn_x[:, par, j], in0=wo_ps[:, D * j:D * j + D],
                                                   scalar=rstd_o[:, par, j:j + 1], in1=x_res[:, par, j],
                                                   op0=mul, op1=add)
                ins.then_inc(attn_x_ready, 1)

            def add_experts(u, par, k):
                dve.wait_ge(attn_x_ready, u + 1)
                dve.wait_ge(y12_ready, u + 1)
                wait(dve, out_out[par], 16 * k)
                dve.tensor_tensor(out_s[:, par], attn_x[:, par], y12[:, par], add).then_inc(sum_ready, 1)

            def inverse_std_o(u, par):
                dve.wait_ge(std_o_ready, u + 1)
                dve.reciprocal(rstd_o[:, par], std_o[:, par]).then_inc(rstd_o_ready, 1)

            def kv_product(u, par, v):
                at = HD * u + v
                if v == 0:
                    dve.wait_ge(kn_ready, u + 1)
                dve.wait_ge(spread_done, at + 1)
                wait(dve, state_ready, at - 1)
                dve.tensor_tensor(kv[:, v % 2], spread_ps[v], k_n[:, par], mul).then_inc(kv_ready, 1)

            def scan(u, par, v):
                at = HD * u + v
                if v == 0:
                    dve.wait_ge(decay_reset, 2 * u + 2)
                dve.wait_ge(kv_ready, at + 1)
                wait(dve, collected, at - 3)
                dve.tensor_tensor_scan(state[:, v % 4], decay[:, par], kv[:, v % 2], 0.0, mul, add
                                       ).then_inc(state_ready, 1)

            def query_state(u, par, v):
                dve.wait_ge(state_ready, HD * u + v + 1)
                dve.tensor_tensor(q_state[:, v % 4], state[:, v % 4], q_s[:, par], mul).then_inc(qs_dve, 1)

            def gate_o(u, par):
                dve.wait_ge(collected, HD * u + HD)
                dve.scalar_tensor_tensor(out=o_s[:, par], in0=gate_t[:, par], scalar=1.0, in1=o_ps[par],
                                         op0=add, op1=mul).then_inc(o_ready, 1)

            def step(u, par, k, first, last):
                for v in range(HD):
                    if v == 7 and not last:
                        norm_keys(u + 1, 1 - par)
                    if v + 1 < HD:
                        kv_product(u, par, v + 1)
                    elif not last:
                        kv_product(u + 1, 1 - par, 0)
                    scan(u, par, v)
                    if v == 0 and not first:
                        query_state(u - 1, 1 - par, HD - 1)
                    if v > 0 and v - 1 in DVE_V:
                        query_state(u, par, v - 1)
                    if v == 1 and not first:
                        gate_o(u - 1, 1 - par)
                    if v == 0 and exists(u - 2):
                        inverse_std_o(u - 2, par)
                    if v == 2 and exists(u - 2):
                        sum_up(u - 2, par, k - 1)
                    if v == 3 and not last:
                        low_v(u + 1, 1 - par)
                    if v == 4 and not first:
                        statistics_o(u - 1, 1 - par)
                    if v == 5 and not first:
                        means_o(u - 1, 1 - par)
                    if v == 6 and exists(u - 2):
                        add_experts(u - 2, par, k - 1)
                    if v == 7 and not last:
                        reset_decay(u + 1, 1 - par)

            assert HD - 1 in DVE_V
            low_v(0, 0)
            norm_keys(0, 0)
            reset_decay(0, 0)
            kv_product(0, 0, 0)
            units_in_steps(dve, step)
            query_state(UNITS - 1, 1, HD - 1)
            gate_o(UNITS - 1, 1)
            statistics_o(UNITS - 1, 1)
            means_o(UNITS - 1, 1)
            for u in (UNITS - 2, UNITS - 1):
                inverse_std_o(u, u % 2)
                sum_up(u, u % 2, u // 2)
                add_experts(u, u % 2, u // 2)

        @block.tensor
        def _(pe):
            def product3(out_ps, w_h, w_l, x_h, x_l):
                pe.matmul(out_ps, w_h, x_h, start=True, stop=False)
                pe.matmul(out_ps, w_h, x_l, start=False, stop=False)
                return pe.matmul(out_ps, w_l, x_h, start=False, stop=True)

            def fold_weights():
                pe.wait_ge(consts_in, 16 * len(EARLY_LOADS))
                pe.matmul(bank[7][:, 0:D], wg1_s[:], wg2t_s[:], start=True, stop=True).then_inc(fold_ps, 1)
                pe.wait_ge(fold, 3)
                pe.matmul(bank[7][:, D:2 * D], center[:], wo_l[:], start=True, stop=True).then_inc(fold_ps, 1)

            def unit_product(out_ps, which, u):
                at = bass.ds(UNIT * u, UNIT)
                return product3(out_ps, proj_hi[:, which], proj_lo[:, which], x_hi[:, at], x_lo[:, at])

            def logits_columns(u, par):
                pe.wait_ge(lo_ready, u + 1)
                wait(pe, logits_t_ready, u - 1)
                unit_product(bank[2 + par], L, u).then_inc(logits_t_done, 1)

            def logits_back(u, par):
                pe.wait_ge(logits_t_ready, u + 1)
                pe.wait_ge(logits_ready, u + 1)
                stand_apart(pe)
                for j in range(UT):
                    ins = pe.transpose(logits_ps[par][:, E * j:E * j + E], logits_t[:, par, P * j:P * j + P],
                                       ident[0:E, 0:E])
                ins.then_inc(logits_done, 1)

            def turn_rows(u, m):
                pe.wait_ge(xn_ready, u + 1)
                wait(pe, lo_ready, u - 1)
                for j in range(UT):
                    ins = pe.transpose(bank[m % 2][:, P * j:P * j + P], xn_rows[:, m, j], ident[:])
                ins.then_inc(turned, 1)

            def step_1(u, m, k):
                if exists(u - 1):
                    turn_rows(u - 1, (m - 1) % 4)
                if exists(u - 2):
                    logits_columns(u - 2, m % 2)
                if exists(u - 3):
                    logits_back(u - 3, (m - 3) % 2)
                if isinstance(u, int) and u == 3:
                    fold_weights()

            pe.wait_ge(proj_in, 16 * len(FIRST_LOADS))
            pe.wait_ge(fold, 2)
            pipeline(pe, step_1)

            def sums_of_squares(u, par):
                pe.wait_ge(sq_ready, u + 1)
                if isinstance(u, int) and u == 0:
                    pe.wait_ge(logits_ready, UNITS + 2)
                for j in range(UT):
                    ins = pe.matmul(squares_ps[:, bass.ds(H * (UT * u + j), H)], k_sq[:, par, P * j:P * j + P],
                                    heads[:], start=True, stop=True)
                ins.then_inc(ss_done, 1)

            def keys_product(u, par):
                wait(pe, k_ready, u - 1)
                unit_product(bank[2 + par], K, u).then_inc(k_done, 1)

            pe.wait_ge(logits_t_ready, UNITS)
            pe.wait_ge(consts_in, 16 * len(EARLY_LOADS))
            for u in range(KEYS_FIRST):
                keys_product(u, u % 2)
                if u > 0:
                    sums_of_squares(u - 1, 1 - u % 2)

            pe.wait_ge(pool_consts, POOL_CONSTS)
            pe.wait_ge(chosen_ready, 1)
            chosen_flat = chosen[:].rearrange("p e t -> p (e t)")
            pe.matmul(bank[0], below[:], chosen_flat, start=True, stop=True)
            pe.matmul(bank[1], ones_b[:], chosen_flat, start=True, stop=True).then_inc(counts_done, 1)
            pe.wait_ge(folded, 2)
            table_ps = bank[7][:, 0:TABLE]
            pe.matmul(table_ps, zero_r[:, 0:P], zero_r[:], start=True, stop=False)

            STEPS = UNITS // 2
            KEYS = (UNITS - KEYS_FIRST) // 2
            with pe.Fori(0, 2) as i:
                done = 0
                for step in range(2 * STEPS):
                    u = STEPS * i + step // 2
                    for m in range(UT * (step % 2), UT * (step % 2) + UT):
                        pe.wait_ge(onehot_ready, 2 * (2 * UT * u + m + 1))
                        pe.matmul(table_ps, is_row[:, m], is_tile[:, m], start=False, stop=False
                                  ).then_inc(onehot_used, 1)
                    if (step + 1) * 2 * KEYS // (2 * STEPS) > done:
                        key, par = KEYS_FIRST + KEYS * i + done // 2, done // 2 % 2
                        if done % 2 == 0:
                            keys_product(key, par)
                        else:
                            sums_of_squares(key - 1, 1 - par)
                        done += 1
            sums_of_squares(UNITS - 1, 1)
            pe.matmul(table_ps, zero_r[:, 0:P], zero_r[:], start=False, stop=True).then_inc(table_done, 1)

            pe.wait_ge(routed, 1)
            pe.wait_ge(len_ready, 1)
            pe.sem_inc(xs_turned, 2)
            pe.sem_inc(down_done, 2)

            def turn_slots(b, h):
                pe.wait_ge(rows_in[h], 32 * b + 32)
                for s in range(SUBS):
                    ins = pe.transpose(bank[6 + h][:, P * s:P * s + P], slot_rows[:, h, s], ident[:])
                ins.then_inc(xs_turned, 1)

            def up(b, h, ep):
                pe.wait_ge(xs_ready, 2 * b + h + 1)
                for c in range(HC):
                    n = (2 * b + h) * HC + c
                    pe.wait_ge(hidden_ready, n + 1)
                    for which, out_ps in ((1, g_ps[c]), (0, h_ps[c])):
                        cols = slice(P * c, P * c + P)
                        ins = product3(out_ps, w_hi[:, ep, which, cols], w_lo[:, ep, which, cols],
                                       xs_hi[:, h], xs_lo[:, h])
                    ins.then_inc(up_done, 1)

            def down(b, h, ep):
                n = 2 * b + h
                pe.wait_ge(hidden_ready, HC * n + 2 * HC)
                pe.wait_ge(y_ready, n + 1)
                for s in range(SUBS):
                    for c in range(HC):
                        ins = pe.matmul(bank[4 + h][:, D * s:D * s + D], hidden[:, h, c, P * s:P * s + P],
                                        w2_s[:, ep, c], start=(c == 0), stop=(c == HC - 1))
                ins.then_inc(down_done, 1)

            for h in range(2):
                turn_slots(0, h)
            with pe.Fori(0, E // 2) as pair:
                for ep in range(2):
                    e = 2 * pair + ep
                    start, end = block_range(pe, e)
                    pe.wait_ge(w_split, e + 1)
                    pe.wait_ge(w2_in[ep], 16 * pair + 16)
                    stand_apart(pe)
                    with pe.Fori(start, end) as b:
                        up(b, 0, ep)
                        up(b, 1, ep)
                        turn_slots(b + 1, 0)
                        down(b, 0, ep)
                        turn_slots(b + 1, 1)
                        down(b, 1, ep)

            pe.wait_ge(experts_over, 1)

            def project(u, i):
                wait(pe, proj_read, 4 * u + i)
                unit_product(proj_ps, (V, Q, F, G)[i], u).then_inc(proj_done, 1)

            def turn_norms(u, par):
                pe.wait_ge(inv_ready_u, u + 1)
                wait(pe, bn_o_ready, u - 1)
                for j in range(UT):
                    rows = inv_u[:, par, H * j:H * j + H].rearrange("p h k -> p (h k)")
                    ins = pe.transpose(turn_ps[:, P * j:P * j + P], rows, ident[:])
                ins.then_inc(inv_turned, 1)

            def spread_v(u, par, v):
                at = HD * u + v
                if v == 0:
                    pe.wait_ge(v_lo_ready, u + 1)
                if v >= 3:
                    pe.wait_ge(kv_ready, at - 2)
                elif v < 2:
                    wait(pe, kv_ready, at - 1)
                pe.matmul(spread_ps[v], spread[:, v], v_hi[:, par], start=True, stop=False)
                pe.matmul(spread_ps[v], spread[:, v], v_lo[:, par], start=False, stop=True
                          ).then_inc(spread_done, 1)

            def collect_v(u, par, v):
                if v in POOL_V:
                    pe.wait_ge(qs_pool, len(POOL_V) * u + POOL_V.index(v) + 1)
                else:
                    pe.wait_ge(qs_dve, len(DVE_V) * u + DVE_V.index(v) + 1)
                if v == 0:
                    wait(pe, o_ready, u - 1)
                pe.matmul(o_ps[par], collect[:, v], q_state[:, v % 4], start=(v == 0), stop=(v == HD - 1)
                          ).then_inc(collected, 1)

            def turn_outputs(u, par):
                pe.wait_ge(o_ready, u + 1)
                wait(pe, kn_ready, u + 1)
                for j in range(UT):
                    ins = pe.transpose(turn_ps[:, D * j:D * j + D], o_s[:, par, P * j:P * j + P], ident[:])
                ins.then_inc(o_turned, 1)

            def output_product(u, par):
                wait(pe, attn_x_ready, u)
                for j in range(UT):
                    ins = pe.matmul(wo_ps[:, D * j:D * j + D], o_s[:, par, P * j:P * j + P], wo_c[:],
                                    start=True, stop=True)
                ins.then_inc(out_done, 1)

            def step(u, par, k, first, last):
                for v in range(HD):
                    if v + 3 < HD:
                        spread_v(u, par, v + 3)
                    elif not last:
                        spread_v(u + 1, 1 - par, v + 3 - HD)
                    collect_v(u, par, v)
                    if v == 1 and not first:
                        turn_outputs(u - 1, 1 - par)
                    if v == 2 and not first:
                        output_product(u - 1, 1 - par)
                    if not last:
                        if v == 0:
                            project(u + 1, 0)
                        if v == 3:
                            project(u + 1, 1)
                        if v == 4:
                            turn_norms(u + 1, 1 - par)
                        if v == 5 or v == 6:
                            project(u + 1, v - 3)

            for i in range(4):
                project(0, i)
            turn_norms(0, 0)
            for v in range(3):
                spread_v(0, 0, v)
            units_in_steps(pe, step)
            turn_outputs(UNITS - 1, 1)
            output_product(UNITS - 1, 1)


def kernel(L0_attn_x, L0_attn_Wq, L0_attn_Wk, L0_attn_Wv, L0_attn_Wf, L0_attn_Wg1, L0_attn_Wg2, L0_attn_ln_w,
           L0_attn_Wo, L0_ffn_Wg, L0_ffn_bg, L0_ffn_W0, L0_ffn_b0, L0_ffn_W1, L0_ffn_b1, L0_ffn_W2, L0_ffn_b2):
    import concourse.bacc as bacc
    from concourse.bass_utils import run_bass_kernel_spmd

    f32 = np.float32
    a = {k: np.asarray(v) for k, v in dict(
        x=L0_attn_x, Wq=L0_attn_Wq, Wk=L0_attn_Wk, Wv=L0_attn_Wv, Wf=L0_attn_Wf, Wg1=L0_attn_Wg1, Wg2=L0_attn_Wg2,
        ln_w=L0_attn_ln_w, Wo=L0_attn_Wo, Wg=L0_ffn_Wg, bg=L0_ffn_bg, W0=L0_ffn_W0, b0=L0_ffn_b0, W1=L0_ffn_W1,
        b1=L0_ffn_b1, W2=L0_ffn_W2, b2=L0_ffn_b2).items()}
    w_proj = np.zeros((D, 5, D), f32)
    w_proj[:, 0] = a["Wq"].T
    w_proj[:, 1] = a["Wk"].T
    w_proj[:, 2] = a["Wv"].T
    w_proj[:, 3] = np.repeat(a["Wf"].T, HD, axis=1)
    w_proj[:, 4, :E] = a["Wg"]
    row, col = np.arange(P)[:, None], np.arange(P)[None, :]
    spread = np.stack([(row == (col // HD) * HD + v) for v in range(HD)], axis=1).astype(f32)
    collect = np.stack([(row // HD == col // HD) & (col % HD == v) for v in range(HD)], axis=1).astype(f32) * f32(0.5)
    token = row + P * np.arange(TILES)[None, :] - T // 2
    arrays = dict(
        x=a["x"].reshape(T, D),
        w_proj=w_proj,
        wg1=a["Wg1"],
        wg2t=a["Wg2"].T,
        wot=a["Wo"].T,
        ln_w=a["ln_w"].reshape(D, 1),
        gate_b=np.broadcast_to(a["bg"].reshape(1, 1, E), (P, UT, E)),
        w0=a["W0"],
        w1=a["W1"],
        w2=a["W2"].reshape(E, HC, P, D).transpose(0, 2, 1, 3),
        b0=a["b0"].reshape(E * HC, P).T,
        b1=a["b1"].reshape(E * HC, P).T,
        b2=np.broadcast_to(a["b2"].reshape(1, E * D), (P, E * D)),
        ident_in=np.eye(P, dtype=f32),
        below_in=(row < col).astype(f32),
        heads_in=(row // HD == np.arange(H)[None, :]).astype(f32),
        spread_in=spread,
        collect_in=collect,
        center_in=np.eye(P, dtype=f32) - f32(1.0 / P),
        iota_in=np.broadcast_to(np.arange(TABLE)[None, :], (P, TABLE)).astype(f32),
        token_in=token.astype(f32),
        rank_in=np.broadcast_to((E - np.arange(E)).reshape(1, E, 1), (P, E, TILES)).astype(f32),
    )
    nc = bacc.Bacc("TRN2", target_bir_lowering=False, num_devices=1)
    args, given = {}, {}
    for name, array in arrays.items():
        given[f"in_{name}"] = np.ascontiguousarray(array)
        args[name] = nc.dram_tensor(f"in_{name}", array.shape, mybir.dt.from_np(array.dtype),
                                    kind="ExternalInput").ap()
    args["out"] = nc.dram_tensor("out_rows", (T, D), F32, kind="ExternalOutput").ap()
    build(nc, **args)
    got = run_bass_kernel_spmd(nc, [given], core_ids=[0]).results[0]["out_rows"]
    return got.reshape(T // SEQ, SEQ, D)
```

```python
from contextlib import ExitStack

import numpy as np

import concourse.bass as bass
from concourse import mybir

F32 = mybir.dt.float32
F32R = mybir.dt.float32r
BF16 = mybir.dt.bfloat16
I32 = mybir.dt.int32
U32 = mybir.dt.uint32
ALU = mybir.AluOpType
ACT = mybir.ActivationFunctionType
AX = mybir.AxisListType

P = 128
D = 128
H = 16
HD = D // H
SEQ = 256
T = 32 * SEQ
TILES = T // P
UNIT = 512
UNITS = T // UNIT
UT = UNIT // P
E = 8
HID = 512
HC = HID // P
BLOCK = 512
HALF = BLOCK // 2
SUBS = HALF // P
MAX_BLOCKS = 2 * T // BLOCK + E - 1
MIN_BLOCKS = 2 * T // BLOCK
TABLE = (MAX_BLOCKS + 1) * BLOCK // P
EPS = 1e-5
NORM_MIN_SQ = 1e-24
POOL_CONSTS = 6 + HD
KEYS_FIRST = 8
POOL_ROWS = (1, 3, 5, 7)
NORM_DVE = 3
POOL_V = (0, 2, 4, 6)
DVE_V = tuple(v for v in range(HD) if v not in POOL_V)
Q, K, V, F, L, G = range(6)


def build(nc, x, w_proj, wg1, wg2t, wot, ln_w, gate_b, w0, w1, w2, b0, b1, b2,
          ident_in, below_in, heads_in, spread_in, collect_in, center_in, iota_in, token_in, rank_in, out):
    xn_dram = nc.dram_tensor("xn_dram", [T, D], F32, kind="Internal").ap()
    y_dram = nc.dram_tensor("y_dram", [MAX_BLOCKS * BLOCK, D], F32, kind="Internal").ap()
    x_units = x.rearrange("(u j p) d -> u p j d", p=P, j=UT)
    xn_units = xn_dram.rearrange("(u j p) d -> u p j d", p=P, j=UT)
    out_units = out.rearrange("(u j p) d -> u p j d", p=P, j=UT)
    y_halves = y_dram.rearrange("(n s p) d -> n p s d", p=P, s=SUBS)

    with ExitStack() as ctx:
        def sb(name, shape, dt=F32, to=ctx):
            return to.enter_context(nc.sbuf_tensor(name, shape, dt))

        def sem(name):
            return ctx.enter_context(nc.semaphore(name))

        psum = ctx.enter_context(nc.psum_tensor("psum", [P, 8, 512], F32))
        bank = [psum[:, i, :] for i in range(8)]
        logits_ps = [psum[:, 4 + i, 0:UT * E] for i in range(2)]
        g_ps, h_ps = ([psum[:, c, first:first + HALF] for c in range(HC)] for first in (0, HALF))
        proj_ps, turn_ps, wo_ps = bank[0], bank[5], bank[6]
        spread_ps = [bank[1 + v % 3] for v in range(HD)]
        o_ps = [bank[4], bank[7]]
        squares_ps = psum[:, 5:7, :].rearrange("p b n -> p (b n)")

        x_hi = sb("x_hi", [P, T], F32R)
        x_lo = sb("x_lo", [P, T], F32R)
        keys = sb("keys", [P, T])
        inv_norm = sb("inv_norm", [P, TILES * H])
        ident = sb("ident", [P, P])
        proj_hi = sb("proj_hi", [P, 6, D], F32R)
        proj_lo = sb("proj_lo", [P, 6, D], F32R)
        wo_c = sb("wo_c", [P, D])
        collect = sb("collect", [P, HD, P])
        spread = sb("spread", [P, HD, P], F32R)
        weight1 = sb("weight1", [P, TILES])
        weight2 = sb("weight2", [P, TILES])
        slots_u = sb("slots_u", [P, 2, TILES], U32)
        token_of = sb("token_of", [P, TABLE], U32)
        tokens_now = sb("tokens_now", [P, 2, SUBS], U32)
        slots_now = sb("slots_now", [P, 2, 2, UT], U32)
        starts = sb("starts", [P, E], I32)
        ends = sb("ends", [P, E], I32)
        k_len = sb("k_len", [P, TILES * H])
        eps_col = sb("eps_col", [P, 1])
        probe = sb("probe", [P, 1])

        early = ExitStack()
        x_rows = sb("x_rows", [P, 4, UT, D], to=early)
        xn_rows = sb("xn_rows", [P, 4, UT, D], to=early)
        spread_raw = sb("spread_raw", [P, HD, P], to=early)
        proj_raw = sb("proj_raw", [P, 5, D], to=early)
        wg1_s = sb("wg1_s", [HD, D], to=early)
        wg2t_s = sb("wg2t_s", [HD, D], to=early)
        wot_s = sb("wot_s", [P, D], to=early)
        wo_l = sb("wo_l", [P, D], to=early)
        lnw_s = sb("lnw_s", [P, 1], to=early)
        center = sb("center", [P, P], to=early)
        heads = sb("heads", [P, H], to=early)
        logits_t = sb("logits_t", [E, 2, UNIT], to=early)
        zeros = sb("zeros", [P, BLOCK // P, D], to=early)
        bn = sb("bn", [P, 4, UT, 6], to=early)
        mean_var = sb("mean_var", [P, 4, UT, 2], to=early)
        std = sb("std", [P, 4, UT], to=early)
        rstd = sb("rstd", [P, 4, UT], to=early)
        k_sq = sb("k_sq", [P, 2, UNIT], to=early)
        ss = sb("ss", [P, TILES * H], to=early)
        bias_g = sb("bias_g", [P, UT, E], to=early)
        rank_c = sb("rank_c", [P, E, TILES], to=early)
        logits = sb("logits", [P, E, TILES], to=early)
        logits2 = sb("logits2", [P, E, TILES], to=early)
        eq = sb("eq", [P, E, TILES], to=early)
        cand = sb("cand", [P, E, TILES], to=early)
        one1 = sb("one1", [P, E, TILES], to=early)
        one2 = sb("one2", [P, E, TILES], to=early)
        chosen = sb("chosen", [P, E, TILES], BF16, to=early)
        top1 = sb("top1", [P, TILES], to=early)
        top2 = sb("top2", [P, TILES], to=early)
        first1 = sb("first1", [P, TILES], to=early)
        first2 = sb("first2", [P, TILES], to=early)
        gap = sb("gap", [P, TILES], to=early)
        e_gap = sb("e_gap", [P, TILES], to=early)
        e_sum = sb("e_sum", [P, TILES], to=early)
        counts = sb("counts", [P, E, TILES], to=early)
        not_first = sb("not_first", [P, E, TILES], to=early)
        upto = sb("upto", [P, E, TILES], to=early)
        place_a = sb("place_a", [P, E, TILES], to=early)
        place_b = sb("place_b", [P, E, TILES], to=early)
        over = sb("over", [P, E, T // BLOCK], to=early)
        blocks_of = sb("blocks_of", [P, E], to=early)
        blocks_min = sb("blocks_min", [P, E], to=early)
        ones_e = sb("ones_e", [P, E], to=early)
        end_f = sb("end_f", [P, E], to=early)
        start_f = sb("start_f", [P, E], to=early)
        picked = sb("picked", [P, E, TILES], to=early)
        slots_f = sb("slots_f", [P, 2, TILES], to=early)
        row_u = sb("row_u", [P, 2, TILES], U32, to=early)
        tile_u = sb("tile_u", [P, 2, TILES], U32, to=early)
        row_f = sb("row_f", [P, 2, TILES], to=early)
        tile_f = sb("tile_f", [P, 2, TILES], to=early)
        iota = sb("iota", [P, TABLE], to=early)
        token_c = sb("token_c", [P, TILES], to=early)
        row_now = sb("row_now", [P, 2, 2, UT], to=early)
        below_raw = sb("below_raw", [P, P], to=early)
        below = sb("below", [P, P], BF16, to=early)
        ones_b = sb("ones_b", [P, P], BF16, to=early)
        zero_r = sb("zero_r", [P, TABLE], F32R, to=early)
        is_row = sb("is_row", [P, 2 * UT, P], F32R, to=early)
        is_tile = sb("is_tile", [P, 2 * UT, TABLE], F32R, to=early)
        early.close()

        mid = ExitStack()
        w_raw = sb("w_raw", [P, 2, 2, HID], to=mid)
        w2_s = sb("w2_s", [P, 2, HC, D], to=mid)
        slot_rows = sb("slot_rows", [P, 2, SUBS, D], to=mid)
        b0_s = sb("b0_s", [P, E * HC], to=mid)
        b1_s = sb("b1_s", [P, E * HC], to=mid)
        b2_s = sb("b2_s", [P, E * D], to=mid)
        xs_hi = sb("xs_hi", [P, 2, HALF], F32R, to=mid)
        xs_lo = sb("xs_lo", [P, 2, HALF], F32R, to=mid)
        y_rows = sb("y_rows", [P, 2, SUBS, D], to=mid)
        w_hi = sb("w_hi", [P, 2, 2, HID], F32R, to=mid)
        w_lo = sb("w_lo", [P, 2, 2, HID], F32R, to=mid)
        gated = sb("gated", [P, HC, HALF], to=mid)
        hidden = sb("hidden", [P, 2, HC, HALF], to=mid)
        mid.close()

        late = ExitStack()
        kv = sb("kv", [P, 2, UNIT], to=late)
        state = sb("state", [P, 4, UNIT], to=late)
        q_state = sb("q_state", [P, HD, UNIT], to=late)
        o_s = sb("o_s", [P, 2, UNIT], to=late)
        bn_o = sb("bn_o", [P, UT, 6], to=late)
        x_res = sb("x_res", [P, 2, UT, D], to=late)
        y1 = sb("y1", [P, 2, UT, D], to=late)
        y2 = sb("y2", [P, 2, UT, D], to=late)
        xy = sb("xy", [P, 2, UT, D], to=late)
        attn = sb("attn", [P, 2, UT, D], to=late)
        q_s = sb("q_s", [P, 2, UNIT], to=late)
        v_s = sb("v_s", [P, 2, UNIT], to=late)
        v_hi = sb("v_hi", [P, 2, UNIT], F32R, to=late)
        v_lo = sb("v_lo", [P, 2, UNIT], F32R, to=late)
        decay_t = sb("decay_t", [P, UNIT], to=late)
        decay = sb("decay", [P, 2, UNIT], to=late)
        gate_t = sb("gate_t", [P, 2, UNIT], to=late)
        k_n = sb("k_n", [P, 2, UNIT], to=late)
        mv_o = sb("mv_o", [P, 2, UT, 2], to=late)
        std_o = sb("std_o", [P, 2, UT], to=late)
        rstd_o = sb("rstd_o", [P, 2, UT], to=late)
        inv_u = sb("inv_u", [P, 2, UT * H, HD], to=late)
        late.close()

        consts_in = sem("consts_in")
        stood = sem("stood")
        early_consts = sem("early_consts")
        proj_in = sem("proj_in")
        pool_consts = sem("pool_consts")
        x_in = [sem(f"x_in{m}") for m in range(4)]
        bn_ready = sem("bn_ready")
        stats_ready = sem("stats_ready")
        std_ready = sem("std_ready")
        rstd_ready = sem("rstd_ready")
        xn_ready = sem("xn_ready")
        xn_pool = sem("xn_pool")
        xn_out = [sem(f"xn_out{m}") for m in range(4)]
        turned = sem("turned")
        hi_ready = sem("hi_ready")
        lo_ready = sem("lo_ready")
        logits_t_done = sem("logits_t_done")
        logits_t_ready = sem("logits_t_ready")
        logits_done = sem("logits_done")
        logits_ready = sem("logits_ready")
        zeros_ready = sem("zeros_ready")
        zeros_out = sem("zeros_out")
        rows_stored = sem("rows_stored")
        fold_ps = sem("fold_ps")
        fold = sem("fold")
        g_hi_ready = sem("g_hi_ready")
        folded = sem("folded")
        k_done = sem("k_done")
        k_ready = sem("k_ready")
        sq_ready = sem("sq_ready")
        ss_done = sem("ss_done")
        ss_ready = sem("ss_ready")
        len_ready = sem("len_ready")
        route = sem("route")
        gap_ready = sem("gap_ready")
        gap_exp = sem("gap_exp")
        chosen_ready = sem("chosen_ready")
        counts_done = sem("counts_done")
        places_ready = sem("places_ready")
        onehot_ready = sem("onehot_ready")
        row_now_ready = sem("row_now_ready")
        pool_row_ready = sem("pool_row_ready")
        onehot_used = sem("onehot_used")
        table_done = sem("table_done")
        ranges_ready = sem("ranges_ready")
        routed = sem("routed")
        raw_in = [sem("raw_in0"), sem("raw_in1")]
        w2_in = [sem("w2_in0"), sem("w2_in1")]
        bias_in = sem("bias_in")
        w_hi_ready = sem("w_hi_ready")
        w_split = sem("w_split")
        inv_ready = sem("inv_ready")
        rows_in = [sem("rows_in0"), sem("rows_in1")]
        xs_turned = sem("xs_turned")
        tokens_ready = sem("tokens_ready")
        slots_ready = sem("slots_ready")
        xs_hi_ready = sem("xs_hi_ready")
        xs_ready = sem("xs_ready")
        up_done = sem("up_done")
        gated_ready = sem("gated_ready")
        hidden_ready = sem("hidden_ready")
        down_done = sem("down_done")
        y_ready = sem("y_ready")
        y_out = [sem("y_out0"), sem("y_out1")]
        experts_over = sem("experts_over")
        proj_done = sem("proj_done")
        proj_read = sem("proj_read")
        v_hi_ready = sem("v_hi_ready")
        v_lo_ready = sem("v_lo_ready")
        decay_ready = sem("decay_ready")
        decay_reset = sem("decay_reset")
        inv_ready_u = sem("inv_ready_u")
        inv_turned = sem("inv_turned")
        kn_ready = sem("kn_ready")
        spread_done = sem("spread_done")
        kv_ready = sem("kv_ready")
        state_ready = sem("state_ready")
        qs_pool = sem("qs_pool")
        qs_dve = sem("qs_dve")
        collected = sem("collected")
        o_ready = sem("o_ready")
        o_turned = sem("o_turned")
        out_done = sem("out_done")
        bn_o_ready = sem("bn_o_ready")
        var_ready = sem("var_ready")
        std_o_ready = sem("std_o_ready")
        rstd_o_ready = sem("rstd_o_ready")
        res_in = [sem("res_in0"), sem("res_in1")]
        y_in = [sem("y_in0"), sem("y_in1")]
        y_scaled = sem("y_scaled")
        rows_added = sem("rows_added")
        xy_ready = sem("xy_ready")
        attn_ready = sem("attn_ready")
        sum_ready = sem("sum_ready")
        out_out = [sem("out_out0"), sem("out_out1")]


        FIRST_LOADS = [(ident, ident_in), (proj_raw, w_proj), (bias_g, gate_b)]
        EARLY_LOADS = [(wg1_s, wg1), (wg2t_s, wg2t),
                       (wot_s, wot), (lnw_s, ln_w), (center, center_in), (heads, heads_in),
                       (spread_raw, spread_in), (collect, collect_in), (rank_c, rank_in),
                       (iota, iota_in), (token_c, token_in), (below_raw, below_in)]

        def wait(eng, semaphore, value):
            if not (isinstance(value, int) and value <= 0):
                eng.wait_ge(semaphore, value)

        def stand_apart(eng):
            eng.sem_inc(stood, 1)

        def units_in_pairs(eng, body):
            for u in range(4):
                body(u, u % 2, u // 2)
            with eng.Fori(2, UNITS // 2) as i:
                body(2 * i, 0, i)
                body(2 * i + 1, 1, i)

        def pipeline(eng, body):
            for u in range(4):
                body(u, u, 0)
            with eng.Fori(1, UNITS // 4) as i:
                for m in range(4):
                    body(4 * i + m, m, i)
            for u in range(UNITS, UNITS + 4):
                body(u, u % 4, u // 4)

        def back(u, m, k, n):
            return u - n, (m - n) % 4, k + (m - n) // 4

        def exists(u):
            return not isinstance(u, int) or 0 <= u < UNITS

        def units_in_steps(eng, step):
            for u in range(5):
                step(u, u % 2, u // 2, u == 0, False)
            with eng.Fori(2, UNITS // 2 - 1) as i:
                step(2 * i + 1, 1, i, False, False)
                step(2 * i + 2, 0, i + 1, False, False)
            step(UNITS - 1, 1, UNITS // 2 - 1, False, True)

        def block_range(eng, e):
            start = eng.value_load(starts[0:1, bass.ds(e, 1)], min_val=0, max_val=MAX_BLOCKS)
            end = eng.value_load(ends[0:1, bass.ds(e, 1)], min_val=1, max_val=MAX_BLOCKS)
            return start, end

        def all_blocks(eng):
            return eng.value_load(ends[0:1, E - 1:E], min_val=1, max_val=MAX_BLOCKS)

        def one(view, i):
            if isinstance(i, int):
                return view[i]
            if len(view.shape) == 4:
                return view[bass.ds(i, 1)].rearrange("u p j d -> (u p) j d")
            return view[bass.ds(i, 1)].rearrange("u p d -> (u p) d")

        def norm_tile(eng, m, j):
            return eng.tensor_scalar(xn_rows[:, m, j], x_rows[:, m, j], mean_var[:, m, j, 0:1],
                                     rstd[:, m, j:j + 1], ALU.subtract, ALU.mult)

        block = ctx.enter_context(nc.Block())

        @block.sync
        def _(sp):
            def load_x(u, m):
                sp.dma_start(x_rows[:, m], one(x_units, u)).then_inc(x_in[m], 16)

            load_x(0, 0)
            for dst, src in FIRST_LOADS:
                sp.dma_start(dst[:], src).then_inc(proj_in, 16)
            for u in range(1, 4):
                load_x(u, u)

            def store_rows(u, m):
                sp.wait_ge(xn_ready, u + 1)
                sp.wait_ge(xn_pool, u + 1)
                sp.dma_start(one(xn_units, u), xn_rows[:, m]).then_inc(xn_out[m], 16)

            def pass_units(i):
                for m in range(4):
                    store_rows(4 * i + m, m)
                    load_x(4 * i + m + 4, m)

            pass_units(0)
            for dst, src in EARLY_LOADS[:6]:
                sp.dma_start(dst[:], src).then_inc(consts_in, 16)
            pass_units(1)
            for dst, src in EARLY_LOADS[6:]:
                sp.dma_start(dst[:], src).then_inc(consts_in, 16)
            pass_units(2)
            for m in range(4):
                store_rows(UNITS - 4 + m, m)
            sp.wait_ge(zeros_ready, 1)
            for b in range(MIN_BLOCKS, MAX_BLOCKS):
                sp.dma_start(y_dram[BLOCK * b:BLOCK * b + BLOCK].rearrange("(j p) d -> p j d", p=P), zeros[:]
                             ).then_inc(zeros_out, 16)
            for m in range(4):
                sp.wait_ge(xn_out[m], 16 * (UNITS // 4))
            sp.wait_ge(zeros_out, 16 * (MAX_BLOCKS - MIN_BLOCKS))
            sp.sem_inc(rows_stored, 1)

            def load_raw(e, par):
                sp.dma_start(w_raw[:, par, 0], one(w0, e)).then_inc(raw_in[par], 16)
                sp.dma_start(w_raw[:, par, 1], one(w1, e)).then_inc(raw_in[par], 16)

            def load_w2(e, par):
                sp.dma_start(w2_s[:, par], one(w2, e)).then_inc(w2_in[par], 16)

            sp.wait_ge(turned, UNITS)
            sp.wait_ge(fold, 3)
            sp.wait_ge(folded, 2)
            sp.wait_ge(pool_consts, POOL_CONSTS)
            load_raw(0, 0)
            load_w2(0, 0)
            for dst, src in ((b0_s, b0), (b1_s, b1), (b2_s, b2)):
                sp.dma_start(dst[:], src).then_inc(bias_in, 16)
            load_raw(1, 1)
            sp.wait_ge(routed, 1)
            for h in range(2):
                sp.sem_inc(y_out[h], 16)
            with sp.Fori(0, E // 2) as pair:
                for ep in range(2):
                    e = 2 * pair + ep
                    start, end = block_range(sp, e)
                    sp.wait_ge(down_done, 2 * start + 2)
                    load_w2((e + 1) % E, 1 - ep)
                    sp.wait_ge(w_split, e + 1)
                    load_raw((e + 2) % E, ep)
                    with sp.Fori(start, end) as b:
                        for h in range(2):
                            sp.wait_ge(y_ready, 2 * b + h + 3)
                            sp.dma_start(one(y_halves, 2 * b + h), y_rows[:, h]).then_inc(y_out[h], 16)
            total = all_blocks(sp)
            for h in range(2):
                sp.wait_ge(y_out[h], 16 * total + 16)
                sp.wait_ge(raw_in[h], 32 * (E // 2 + 1))
                sp.wait_ge(rows_in[h], 32 * total + 32)
            sp.wait_ge(w2_in[0], 16 * (E // 2 + 1))
            sp.wait_ge(w_split, E + 1)
            sp.wait_ge(xs_ready, 2 * total + 2)
            sp.sem_inc(experts_over, 1)

            def load_res(u, par):
                wait(sp, xy_ready, u - 1)
                sp.dma_start(x_res[:, par], one(x_units, u)).then_inc(res_in[par], 16)

            def store(u, par):
                sp.wait_ge(sum_ready, u + 1)
                sp.dma_start(one(out_units, u), attn[:, par]).then_inc(out_out[par], 16)

            load_res(0, 0)
            load_res(1, 1)
            with sp.Fori(0, UNITS // 2 - 1) as i:
                for par in range(2):
                    store(2 * i + par, par)
                    load_res(2 * i + par + 2, par)
            store(UNITS - 2, 0)
            store(UNITS - 1, 1)
            for par in range(2):
                sp.wait_ge(out_out[par], 16 * (UNITS // 2))

        @block.gpsimd
        def _(pool):
            pool.memset(zeros[:], 0.0).then_inc(zeros_ready, 1)
            def step_1(u, m, k):
                if exists(u - 1):
                    n, m, k = back(u, m, k, 1)
                    pool.wait_ge(rstd_ready, n + 1)
                    wait(pool, turned, n - 3)
                    wait(pool, xn_out[m], 16 * k)
                    stand_apart(pool)
                    for j in range(NORM_DVE, UT):
                        ins = norm_tile(pool, m, j)
                    ins.then_inc(xn_pool, 1)

            pipeline(pool, step_1)

            pool.memset(ones_b[:], 1.0).then_inc(pool_consts, 1)
            pool.memset(ones_e[:], 1.0).then_inc(pool_consts, 1)
            pool.memset(not_first[:, :, 1:TILES], 1.0).then_inc(pool_consts, 1)
            pool.memset(not_first[:, :, 0:1], 0.0).then_inc(pool_consts, 1)
            pool.wait_ge(zeros_ready, 1)
            pool.tensor_copy(zero_r[:], zeros[:].rearrange("p j d -> p (j d)")[:, 0:TABLE]).then_inc(pool_consts, 1)
            pool.wait_ge(consts_in, 16 * len(EARLY_LOADS))
            pool.tensor_copy(below[:], below_raw[:]).then_inc(pool_consts, 1)
            for v in range(HD):
                pool.tensor_copy(spread[:, v], spread_raw[:, v]).then_inc(pool_consts, 1)

            def one_hot_rows(u, par):
                n = len(POOL_ROWS)
                pool.wait_ge(pool_row_ready, n * u + n)
                pool.tensor_copy(row_now[:, par], row_f[:, :, bass.ds(UT * u, UT)]).then_inc(row_now_ready, 1)
                pool.wait_ge(row_now_ready, u + 1)
                for m in POOL_ROWS:
                    pool.wait_ge(onehot_used, 2 * UT * u + m + 1)
                    stand_apart(pool)
                    pool.tensor_scalar(is_row[:, m], iota[:, 0:P], row_now[:, par, m % 2, m // 2:m // 2 + 1], None,
                                       ALU.is_equal).then_inc(pool_row_ready, 1)

            pool.sem_inc(pool_row_ready, 2 * len(POOL_ROWS))
            pool.wait_ge(places_ready, 1)
            with pool.Fori(0, UNITS // 2) as i:
                for par in range(2):
                    one_hot_rows(2 * i + par, par)

            pool.wait_ge(ranges_ready, 2)
            total = all_blocks(pool)
            pool.wait_ge(turned, UNITS)
            pool.wait_ge(rows_stored, 1)
            pool.wait_ge(routed, 1)
            with pool.Fori(0, total + 1) as b:
                for h in range(2):
                    pool.wait_ge(xs_turned, 2 * b + h + 1)
                    at = bass.ds((2 * b + h) * SUBS, SUBS)
                    pool.tensor_copy(tokens_now[:, h], token_of[:, at]).then_inc(tokens_ready, 1)
                    pool.wait_ge(tokens_ready, 2 * b + h + 1)
                    stand_apart(pool)
                    for s in range(SUBS):
                        pool.indirect_dma_start(slot_rows[:, h, s], None, xn_dram,
                                                bass.IndirectOffsetOnAxis(tokens_now[:, h, s:s + 1], 0)
                                                ).then_inc(rows_in[h], 16)

            pool.wait_ge(experts_over, 1)

            def add_rows(u, par):
                pool.wait_ge(y_scaled, u + 1)
                pool.tensor_tensor(y1[:, par], y1[:, par], y2[:, par], ALU.add).then_inc(rows_added, 1)

            def add_x(u, par, k):
                pool.wait_ge(rows_added, u + 1)
                pool.wait_ge(res_in[par], 16 * (k + 1))
                wait(pool, sum_ready, u - 1)
                pool.tensor_tensor(xy[:, par], y1[:, par], x_res[:, par], ALU.add).then_inc(xy_ready, 1)

            def step(u, par, k, first, last):
                wait(pool, xy_ready, u - 1)
                pool.tensor_copy(slots_now[:, par], slots_u[:, :, bass.ds(UT * u, UT)]).then_inc(slots_ready, 1)
                pool.wait_ge(slots_ready, u + 1)
                pool.wait_ge(proj_read, 4 * u + 3)
                for n, v in enumerate(POOL_V):
                    pool.wait_ge(state_ready, HD * u + v + 1)
                    wait(pool, collected, HD * u + v - 7)
                    pool.tensor_tensor(q_state[:, v], state[:, v % 4], q_s[:, par], ALU.mult
                                       ).then_inc(qs_pool, 1)
                    for choice, rows in ((0, y1), (1, y2)):
                        pool.indirect_dma_start(
                            rows[:, par, n], None, y_dram,
                            bass.IndirectOffsetOnAxis(slots_now[:, par, choice, n:n + 1], 0),
                        ).then_inc(y_in[par], 16)
                    if n == 2 and not first:
                        add_rows(u - 1, 1 - par)
                    if n == 3 and not first:
                        add_x(u - 1, 1 - par, k if par else k - 1)

            assert len(POOL_V) == UT
            units_in_steps(pool, step)
            add_rows(UNITS - 1, 1)
            add_x(UNITS - 1, 1, UNITS // 2 - 1)

        @block.scalar
        def _(act):
            act.wait_ge(early_consts, 1)
            act.activation(probe[:, 0:1], eps_col[:, 0:1], ACT.Sqrt)

            def std_of(u, m):
                act.wait_ge(stats_ready, u + 1)
                wait(act, rstd_ready, u - 3)
                act.activation(std[:, m], mean_var[:, m, :, 1], ACT.Sqrt, bias=eps_col[:, 0:1]
                               ).then_inc(std_ready, 1)

            def high_part(u, par):
                act.wait_ge(turned, u + 1)
                stand_apart(act)
                act.activation(x_hi[:, bass.ds(UNIT * u, UNIT)], bank[par][:, :], ACT.Copy).then_inc(hi_ready, 1)

            def logits_row(u, par):
                act.wait_ge(logits_t_done, u + 1)
                wait(act, logits_done, u - 1)
                act.activation(logits_t[:, par], bank[2 + par][0:E, :], ACT.Copy).then_inc(logits_t_ready, 1)

            def step_1(u, m, k):
                if exists(u):
                    std_of(u, m)
                if exists(u - 1):
                    high_part(u - 1, (m - 1) % 2)
                if exists(u - 2):
                    logits_row(u - 2, m % 2)

            pipeline(act, step_1)

            def key_unit(u, par, k):
                act.wait_ge(k_done, u + 1)
                stand_apart(act)
                act.activation(keys[:, bass.ds(UNIT * u, UNIT)], bank[2 + par][:, :], ACT.Silu).then_inc(k_ready, 1)
                act.wait_ge(k_ready, u + 1)
                wait(act, ss_done, u - 1)
                stand_apart(act)
                act.activation(k_sq[:, par], keys[:, bass.ds(UNIT * u, UNIT)], ACT.Square).then_inc(sq_ready, 1)

            for u in range(KEYS_FIRST // 2):
                key_unit(u, u % 2, u // 2)
            act.wait_ge(gap_ready, 1)
            act.activation(e_gap[:], gap[:], ACT.Exp).then_inc(gap_exp, 1)
            for u in range(KEYS_FIRST // 2, KEYS_FIRST):
                key_unit(u, u % 2, u // 2)
            with act.Fori(KEYS_FIRST // 2, UNITS // 2) as i:
                key_unit(2 * i, 0, i)
                key_unit(2 * i + 1, 1, i)
            act.wait_ge(ss_ready, 2)
            act.activation(k_len[:], ss[:], ACT.Sqrt).then_inc(len_ready, 1)

            def load_silu_table():
                act.activation(probe[:, 0:1], eps_col[:, 0:1], ACT.Silu)

            act.wait_ge(routed, 1)
            act.wait_ge(bias_in, 48)

            def xs_high_part(n, h):
                act.wait_ge(xs_turned, n + 3)
                act.activation(xs_hi[:, h], bank[6 + h][:, 0:HALF], ACT.Copy).then_inc(xs_hi_ready, 1)

            def weights_high_part(s, par, k):
                act.wait_ge(raw_in[par], 32 * (k + 1))
                for i in range(2):
                    act.activation(w_hi[:, par, i], w_raw[:, par, i], ACT.Copy).then_inc(w_hi_ready, 1)

            weights_high_part(0, 0, 0)
            for h in range(2):
                xs_high_part(h, h)
            def gate_block(b, e):
                load_silu_table()
                for h in range(2):
                    for c in range(HC):
                        n = (2 * b + h) * HC + c
                        act.wait_ge(up_done, n + 1)
                        act.wait_ge(hidden_ready, n + 1)
                        stand_apart(act)
                        act.activation(gated[:, c], g_ps[c], ACT.Silu,
                                       bias=b1_s[:, bass.ds(HC * e + c, 1)]).then_inc(gated_ready, 1)
                for h in range(2):
                    xs_high_part(2 * b + 2 + h, h)

            with act.Fori(0, E // 2) as pair:
                for ep in range(2):
                    e = 2 * pair + ep
                    start, end = block_range(act, e)
                    gate_block(start, e)
                    weights_high_part(e + 1, 1 - ep, pair + ep)
                    with act.If(start + 1 < end):
                        with act.Fori(start + 1, end) as b:
                            gate_block(b, e)


            def head_1(u, par):
                wait(act, o_ready, u - 1)
                stand_apart(act)
                act.activation(inv_u[:, par], inv_norm[:, bass.ds(UT * H * u, UT * H)].unsqueeze(2)
                               .broadcast_to([P, UT * H, HD]), ACT.Copy).then_inc(inv_ready_u, 1)
                act.wait_ge(proj_done, 4 * u + 1)
                act.activation(v_s[:, par], proj_ps, ACT.Silu).then_inc(proj_read, 1)
                act.wait_ge(proj_read, 4 * u + 1)
                act.activation(v_hi[:, par], v_s[:, par], ACT.Copy).then_inc(v_hi_ready, 1)
                act.wait_ge(proj_done, 4 * u + 2)
                wait(act, decay_ready, u)
                act.activation(decay_t[:], proj_ps, ACT.Tanh, scale=0.5).then_inc(proj_read, 1)
                act.wait_ge(proj_read, 4 * u + 2)
                act.activation(decay[:, par], decay_t[:], ACT.Copy, scale=0.5, bias=0.5).then_inc(decay_ready, 1)

            def head_2(u, par):
                act.wait_ge(proj_done, 4 * u + 3)
                act.activation(q_s[:, par], proj_ps, ACT.Silu).then_inc(proj_read, 1)
                act.wait_ge(proj_done, 4 * u + 4)
                act.activation(gate_t[:, par], proj_ps, ACT.Tanh, scale=0.5).then_inc(proj_read, 1)

            def weight_rows(u, par, k):
                act.wait_ge(y_in[par], 16 * 2 * UT * (k + 1))
                stand_apart(act)
                for j in range(UT):
                    for rows, weight in ((y1, weight1), (y2, weight2)):
                        ins = act.activation(rows[:, par, j], rows[:, par, j], ACT.Copy,
                                             scale=weight[:, bass.ds(UT * u + j, 1)])
                ins.then_inc(y_scaled, 1)

            def std_of_o(u, par):
                act.wait_ge(var_ready, u + 1)
                wait(act, rstd_o_ready, u - 1)
                act.activation(std_o[:, par], mv_o[:, par, :, 1], ACT.Sqrt, bias=eps_col[:, 0:1]
                               ).then_inc(std_o_ready, 1)

            def scale_outputs(u, par, k):
                act.wait_ge(rstd_o_ready, u + 1)
                act.wait_ge(out_done, u + 1)
                wait(act, out_out[par], 16 * k)
                for j in range(UT):
                    ins = act.activation(attn[:, par, j], wo_ps[:, D * j:D * j + D], ACT.Copy,
                                         scale=rstd_o[:, par, j:j + 1])
                ins.then_inc(attn_ready, 1)

            def step(u, par, k, first, last):
                if not last:
                    load_silu_table()
                if not last:
                    head_1(u + 1, 1 - par)
                if exists(u - 2):
                    scale_outputs(u - 2, par, k - 1)
                if not first:
                    weight_rows(u - 1, 1 - par, k if par else k - 1)
                if not last:
                    head_2(u + 1, 1 - par)
                if not first:
                    std_of_o(u - 1, 1 - par)

            head_1(0, 0)
            head_2(0, 0)
            act.wait_ge(experts_over, 1)
            units_in_steps(act, step)
            scale_outputs(UNITS - 2, 0, UNITS // 2 - 1)
            weight_rows(UNITS - 1, 1, UNITS // 2 - 1)
            std_of_o(UNITS - 1, 1)
            scale_outputs(UNITS - 1, 1, UNITS // 2 - 1)

        @block.vector
        def _(dve):
            sub, mul, add = ALU.subtract, ALU.mult, ALU.add
            dve.memset(eps_col[:], EPS).then_inc(early_consts, 1)
            dve.sem_inc(logits_ready, 2)

            def statistics(u, m, k):
                dve.wait_ge(x_in[m], 16 * (k + 1))
                wait(dve, xn_ready, u - 3)
                wait(dve, xn_pool, u - 3)
                for j in range(UT):
                    ins = dve.bn_stats(bn[:, m, j], x_rows[:, m, j])
                ins.then_inc(bn_ready, 1)

            def means(u, m):
                dve.wait_ge(bn_ready, u + 1)
                stand_apart(dve)
                for j in range(UT):
                    ins = dve.bn_aggr(mean_var[:, m, j], bn[:, m, j])
                ins.then_inc(stats_ready, 1)

            def inverse_std(u, m):
                dve.wait_ge(std_ready, u + 1)
                dve.reciprocal(rstd[:, m], std[:, m]).then_inc(rstd_ready, 1)

            def norm_rows(u, m, k):
                dve.wait_ge(rstd_ready, u + 1)
                wait(dve, turned, u - 3)
                wait(dve, xn_out[m], 16 * k)
                for j in range(NORM_DVE):
                    ins = norm_tile(dve, m, j)
                ins.then_inc(xn_ready, 1)

            def low_part(u, par):
                at = bass.ds(UNIT * u, UNIT)
                dve.wait_ge(hi_ready, u + 1)
                dve.tensor_tensor(x_lo[:, at], bank[par][:, :], x_hi[:, at].bitcast(F32), sub).then_inc(lo_ready, 1)

            def take_logits(u, par):
                dve.wait_ge(logits_done, u + 1)
                dve.tensor_tensor(logits[:, :, bass.ds(UT * u, UT)].rearrange("p e j -> p j e"),
                                  logits_ps[par].rearrange("p (j e) -> p j e", e=E), bias_g[:], add
                                  ).then_inc(logits_ready, 1)

            def step_1(u, m, k):
                if exists(u):
                    statistics(u, m, k)
                if exists(u - 1):
                    inverse_std(u - 1, (m - 1) % 4)
                if exists(u):
                    means(u, m)
                if exists(u - 1):
                    norm_rows(*back(u, m, k, 1))
                if isinstance(u, int) and u == 1:
                    split_projections()
                if exists(u - 2):
                    low_part(u - 2, m % 2)
                if isinstance(u, int) and u == UNITS + 1:
                    fold_weights()
                if exists(u - 4):
                    take_logits(u - 4, m % 2)

            def split_projections():
                dve.wait_ge(proj_in, 16 * len(FIRST_LOADS))
                dve.tensor_copy(proj_hi[:, 0:G], proj_raw[:]).then_inc(fold, 1)
                dve.wait_ge(fold, 1)
                dve.tensor_tensor(proj_lo[:, 0:G], proj_raw[:], proj_hi[:, 0:G].bitcast(F32), sub).then_inc(fold, 1)

            def fold_weights():
                dve.wait_ge(consts_in, 16 * len(EARLY_LOADS))
                dve.tensor_scalar(wo_l[:], wot_s[:], lnw_s[:, 0:1], None, mul).then_inc(fold, 1)
                dve.wait_ge(fold_ps, 2)
                dve.tensor_copy(proj_hi[:, G], bank[7][:, 0:D]).then_inc(g_hi_ready, 1)
                dve.wait_ge(g_hi_ready, 1)
                dve.tensor_tensor(proj_lo[:, G], bank[7][:, 0:D], proj_hi[:, G].bitcast(F32), sub).then_inc(folded, 1)
                dve.tensor_copy(wo_c[:], bank[7][:, D:2 * D]).then_inc(folded, 1)

            pipeline(dve, step_1)

            n_route = [0]

            def step_done(ins):
                n_route[0] += 1
                ins.then_inc(route, 1)
                dve.wait_ge(route, n_route[0])

            def over_experts(a):
                return a.unsqueeze(1).broadcast_to([P, E, TILES])

            dve.wait_ge(pool_consts, POOL_CONSTS)
            dve.wait_ge(logits_ready, UNITS + 2)
            source = logits
            for top, first_e, pick in ((top1, first1, one1), (top2, first2, one2)):
                step_done(dve.tensor_reduce(top[:], source[:].rearrange("p e t -> p t e"), AX.X, ALU.max))
                if source is logits2:
                    step_done(dve.tensor_tensor(gap[:], top2[:], top1[:], sub))
                    dve.sem_inc(gap_ready, 1)
                step_done(dve.tensor_tensor(eq[:], source[:], over_experts(top[:]), ALU.is_equal))
                step_done(dve.tensor_tensor(cand[:], eq[:], rank_c[:], mul))
                step_done(dve.tensor_reduce(first_e[:], cand[:].rearrange("p e t -> p t e"), AX.X, ALU.max))
                step_done(dve.tensor_tensor(pick[:], cand[:], over_experts(first_e[:]), ALU.is_equal))
                if source is logits:
                    step_done(dve.scalar_tensor_tensor(out=logits2[:], in0=pick[:], scalar=-3e38, in1=logits[:],
                                                       op0=mul, op1=add))
                    source = logits2
            dve.tensor_tensor(chosen[:], one1[:], one2[:], add).then_inc(chosen_ready, 1)
            dve.wait_ge(counts_done, 1)
            step_done(dve.tensor_copy(counts[:].rearrange("p e t -> p (e t)"), bank[1][:, :]))
            step_done(dve.tensor_tensor_scan(upto[:].rearrange("p e t -> p (e t)"),
                                             not_first[:].rearrange("p e t -> p (e t)"),
                                             counts[:].rearrange("p e t -> p (e t)"), 0.0, mul, add))
            step_done(dve.scalar_tensor_tensor(
                out=over[:], in0=upto[:, :, TILES - 1:TILES].broadcast_to([P, E, T // BLOCK]), scalar=1.0 / BLOCK,
                in1=iota[:, 0:T // BLOCK].unsqueeze(1).broadcast_to([P, E, T // BLOCK]), op0=mul, op1=ALU.is_gt))
            step_done(dve.tensor_reduce(blocks_of[:], over[:], AX.X, add))
            step_done(dve.tensor_scalar(blocks_min[:], blocks_of[:], 1.0, None, ALU.max))
            step_done(dve.tensor_tensor_scan(end_f[:], ones_e[:], blocks_min[:], 0.0, mul, add))
            step_done(dve.tensor_tensor(start_f[:], end_f[:], blocks_min[:], sub))
            dve.tensor_copy(ends[:], end_f[:]).then_inc(ranges_ready, 1)
            dve.tensor_copy(starts[:], start_f[:]).then_inc(ranges_ready, 1)
            step_done(dve.tensor_tensor(place_a[:], upto[:], counts[:], sub))
            step_done(dve.tensor_tensor(place_b[:].rearrange("p e t -> p (e t)"), bank[0][:, :],
                                        place_a[:].rearrange("p e t -> p (e t)"), add))
            step_done(dve.scalar_tensor_tensor(out=place_a[:], in0=start_f[:].unsqueeze(2).broadcast_to([P, E, TILES]),
                                               scalar=float(BLOCK), in1=place_b[:], op0=mul, op1=add))
            for choice, pick in ((0, one1), (1, one2)):
                step_done(dve.tensor_tensor(picked[:], pick[:], place_a[:], mul))
                step_done(dve.tensor_reduce(slots_f[:, choice], picked[:].rearrange("p e t -> p t e"), AX.X, add))
            step_done(dve.tensor_copy(slots_u[:], slots_f[:]))
            step_done(dve.tensor_scalar(row_u[:], slots_u[:], P - 1, None, ALU.bitwise_and))
            step_done(dve.tensor_scalar(tile_u[:], slots_u[:], 7, None, ALU.logical_shift_right))
            step_done(dve.tensor_copy(row_f[:], row_u[:]))
            dve.sem_inc(places_ready, 1)
            step_done(dve.tensor_copy(tile_f[:], tile_u[:]))

            def one_hots(u, par, k):
                for m in range(2 * UT):
                    j, choice = m // 2, m % 2
                    t = UT * u + j
                    row, tile = (a[:, choice, bass.ds(t, 1)] for a in (row_f, tile_f))
                    dve.wait_ge(onehot_used, 2 * UT * u + m + 1)
                    if m not in POOL_ROWS:
                        dve.tensor_scalar(is_row[:, m], iota[:, 0:P], row, None, ALU.is_equal)
                    dve.tensor_scalar(is_tile[:, m], iota[:], tile, token_c[:, bass.ds(t, 1)],
                                      ALU.is_equal, mul).then_inc(onehot_ready, 1)

            units_in_pairs(dve, one_hots)
            dve.wait_ge(gap_exp, 1)
            step_done(dve.tensor_scalar(e_sum[:], e_gap[:], 1.0, None, add))
            step_done(dve.reciprocal(weight1[:], e_sum[:]))
            step_done(dve.tensor_tensor(weight2[:], e_gap[:], weight1[:], mul))
            dve.wait_ge(table_done, 1)
            dve.tensor_scalar(token_of[:], bank[7][:, 0:TABLE], float(T // 2), None, add).then_inc(routed, 1)

            dve.wait_ge(ss_done, UNITS)
            for i in range(2):
                dve.tensor_scalar(ss[:, 512 * i:512 * i + 512], bank[5 + i][:, :], NORM_MIN_SQ, None, ALU.max
                                  ).then_inc(ss_ready, 1)

            dve.wait_ge(routed, 1)
            dve.wait_ge(len_ready, 1)
            dve.wait_ge(bias_in, 48)
            dve.sem_inc(hidden_ready, HC)
            dve.sem_inc(y_ready, 2)

            def split_weights(s, par):
                for i in range(2):
                    dve.wait_ge(w_hi_ready, 2 * s + i + 1)
                    ins = dve.tensor_tensor(w_lo[:, par, i], w_raw[:, par, i], w_hi[:, par, i].bitcast(F32), sub)
                ins.then_inc(w_split, 1)

            def xs_low_part(n, h):
                dve.wait_ge(xs_hi_ready, n + 1)
                dve.tensor_tensor(xs_lo[:, h], bank[6 + h][:, 0:HALF], xs_hi[:, h].bitcast(F32), sub
                                  ).then_inc(xs_ready, 1)

            def finish_block(b, e):
                for h in range(2):
                    dve.wait_ge(down_done, 2 * b + h + 1)
                    for c in range(HC):
                        dve.wait_ge(gated_ready, (2 * b + h) * HC + c + 1)
                        dve.scalar_tensor_tensor(out=hidden[:, h, c], in0=h_ps[c],
                                                 scalar=b0_s[:, bass.ds(HC * e + c, 1)],
                                                 in1=gated[:, c], op0=add, op1=mul).then_inc(hidden_ready, 1)
                for h in range(2):
                    n = 2 * b + h
                    xs_low_part(n + 2, h)
                    dve.wait_ge(down_done, n + 3)
                    dve.wait_ge(y_out[h], 16 * b + 16)
                    for s in range(SUBS):
                        ins = dve.tensor_tensor(y_rows[:, h, s], bank[4 + h][:, D * s:D * s + D],
                                                b2_s[:, bass.ds(D * e, D)], add)
                    ins.then_inc(y_ready, 1)

            split_weights(0, 0)
            for h in range(2):
                xs_low_part(h, h)
            with dve.Fori(0, E // 2) as pair:
                for ep in range(2):
                    e = 2 * pair + ep
                    start, end = block_range(dve, e)
                    share = bass.ds(TILES * H // E * e, TILES * H // E)
                    dve.reciprocal(inv_norm[:, share], k_len[:, share]).then_inc(inv_ready, 1)
                    finish_block(start, e)
                    split_weights(e + 1, 1 - ep)
                    with dve.If(start + 1 < end):
                        with dve.Fori(start + 1, end) as b:
                            finish_block(b, e)


            def low_v(u, par):
                wait(dve, o_ready, u - 1)
                dve.wait_ge(v_hi_ready, u + 1)
                dve.tensor_tensor(v_lo[:, par], v_s[:, par], v_hi[:, par].bitcast(F32), sub).then_inc(v_lo_ready, 1)

            def reset_decay(u, par):
                dve.wait_ge(decay_ready, u + 1)
                for s in range(UNIT // SEQ):
                    dve.memset(decay[:, par, SEQ * s:SEQ * s + 1], 0.0).then_inc(decay_reset, 1)

            def norm_keys(u, par):
                dve.wait_ge(inv_turned, u + 1)
                dve.tensor_tensor(k_n[:, par], turn_ps, keys[:, bass.ds(UNIT * u, UNIT)], mul
                                  ).then_inc(kn_ready, 1)

            def statistics_o(u, par):
                dve.wait_ge(o_turned, u + 1)
                wait(dve, std_o_ready, u - 1)
                wait(dve, var_ready, u)
                for j in range(UT):
                    ins = dve.bn_stats(bn_o[:, j], turn_ps[:, D * j:D * j + D])
                ins.then_inc(bn_o_ready, 1)

            def means_o(u, par):
                dve.wait_ge(bn_o_ready, u + 1)
                stand_apart(dve)
                for j in range(UT):
                    ins = dve.bn_aggr(mv_o[:, par, j], bn_o[:, j])
                ins.then_inc(var_ready, 1)

            def sum_up(u, par):
                dve.wait_ge(attn_ready, u + 1)
                dve.wait_ge(xy_ready, u + 1)
                dve.tensor_tensor(attn[:, par], attn[:, par], xy[:, par], add).then_inc(sum_ready, 1)

            def inverse_std_o(u, par):
                dve.wait_ge(std_o_ready, u + 1)
                dve.reciprocal(rstd_o[:, par], std_o[:, par]).then_inc(rstd_o_ready, 1)

            def kv_product(u, par, v):
                at = HD * u + v
                if v == 0:
                    dve.wait_ge(kn_ready, u + 1)
                dve.wait_ge(spread_done, at + 1)
                wait(dve, state_ready, at - 1)
                dve.tensor_tensor(kv[:, v % 2], spread_ps[v], k_n[:, par], mul).then_inc(kv_ready, 1)

            def scan(u, par, v):
                at = HD * u + v
                if v == 0:
                    dve.wait_ge(decay_reset, 2 * u + 2)
                dve.wait_ge(kv_ready, at + 1)
                if v in POOL_V:
                    wait(dve, qs_pool, len(POOL_V) * u + POOL_V.index(v) - 1)
                else:
                    wait(dve, qs_dve, len(DVE_V) * u + DVE_V.index(v) - 1)
                dve.tensor_tensor_scan(state[:, v % 4], decay[:, par], kv[:, v % 2], 0.0, mul, add
                                       ).then_inc(state_ready, 1)

            def query_state(u, par, v):
                dve.wait_ge(state_ready, HD * u + v + 1)
                if v == DVE_V[0]:
                    dve.wait_ge(proj_read, 4 * u + 3)
                wait(dve, collected, HD * u + v - 7)
                dve.tensor_tensor(q_state[:, v], state[:, v % 4], q_s[:, par], mul).then_inc(qs_dve, 1)

            def gate_o(u, par):
                dve.wait_ge(collected, HD * u + HD)
                dve.wait_ge(proj_read, 4 * u + 4)
                dve.scalar_tensor_tensor(out=o_s[:, par], in0=gate_t[:, par], scalar=1.0, in1=o_ps[par],
                                         op0=add, op1=mul).then_inc(o_ready, 1)

            def step(u, par, k, first, last):
                for v in range(HD):
                    if v == 7 and not last:
                        norm_keys(u + 1, 1 - par)
                    if v + 1 < HD:
                        kv_product(u, par, v + 1)
                    elif not last:
                        kv_product(u + 1, 1 - par, 0)
                    scan(u, par, v)
                    if v == 0 and not first:
                        query_state(u - 1, 1 - par, HD - 1)
                    if v > 0 and v - 1 in DVE_V:
                        query_state(u, par, v - 1)
                    if v == 1 and not first:
                        gate_o(u - 1, 1 - par)
                    if v == 1 and exists(u - 2):
                        inverse_std_o(u - 2, par)
                    if v == 6 and exists(u - 2):
                        sum_up(u - 2, par)
                    if v == 3 and not last:
                        low_v(u + 1, 1 - par)
                    if v == 4 and not first:
                        statistics_o(u - 1, 1 - par)
                    if v == 5 and not first:
                        means_o(u - 1, 1 - par)
                    if v == 7 and not last:
                        reset_decay(u + 1, 1 - par)

            assert HD - 1 in DVE_V
            low_v(0, 0)
            norm_keys(0, 0)
            reset_decay(0, 0)
            dve.wait_ge(experts_over, 1)
            kv_product(0, 0, 0)
            units_in_steps(dve, step)
            inverse_std_o(UNITS - 2, 0)
            query_state(UNITS - 1, 1, HD - 1)
            gate_o(UNITS - 1, 1)
            statistics_o(UNITS - 1, 1)
            means_o(UNITS - 1, 1)
            inverse_std_o(UNITS - 1, 1)
            for u in (UNITS - 2, UNITS - 1):
                sum_up(u, u % 2)

        @block.tensor
        def _(pe):
            def product3(out_ps, w_h, w_l, x_h, x_l):
                pe.matmul(out_ps, w_h, x_h, start=True, stop=False)
                pe.matmul(out_ps, w_h, x_l, start=False, stop=False)
                return pe.matmul(out_ps, w_l, x_h, start=False, stop=True)

            def fold_weights():
                pe.wait_ge(consts_in, 16 * len(EARLY_LOADS))
                pe.matmul(bank[7][:, 0:D], wg1_s[:], wg2t_s[:], start=True, stop=True).then_inc(fold_ps, 1)
                pe.wait_ge(fold, 3)
                pe.matmul(bank[7][:, D:2 * D], center[:], wo_l[:], start=True, stop=True).then_inc(fold_ps, 1)

            def unit_product(out_ps, which, u):
                at = bass.ds(UNIT * u, UNIT)
                return product3(out_ps, proj_hi[:, which], proj_lo[:, which], x_hi[:, at], x_lo[:, at])

            def logits_columns(u, par):
                pe.wait_ge(lo_ready, u + 1)
                wait(pe, logits_t_ready, u - 1)
                unit_product(bank[2 + par], L, u).then_inc(logits_t_done, 1)

            def logits_back(u, par):
                pe.wait_ge(logits_t_ready, u + 1)
                pe.wait_ge(logits_ready, u + 1)
                stand_apart(pe)
                for j in range(UT):
                    ins = pe.transpose(logits_ps[par][:, E * j:E * j + E], logits_t[:, par, P * j:P * j + P],
                                       ident[0:E, 0:E])
                ins.then_inc(logits_done, 1)

            def turn_rows(u, m):
                pe.wait_ge(xn_ready, u + 1)
                pe.wait_ge(xn_pool, u + 1)
                wait(pe, lo_ready, u - 1)
                for j in range(UT):
                    ins = pe.transpose(bank[m % 2][:, P * j:P * j + P], xn_rows[:, m, j], ident[:])
                ins.then_inc(turned, 1)

            def step_1(u, m, k):
                if exists(u - 1):
                    turn_rows(u - 1, (m - 1) % 4)
                if isinstance(u, int) and u == 2:
                    pe.wait_ge(fold, 2)
                if exists(u - 2):
                    logits_columns(u - 2, m % 2)
                if exists(u - 3):
                    logits_back(u - 3, (m - 3) % 2)
                if isinstance(u, int) and u == UNITS + 1:
                    fold_weights()

            pe.sem_inc(onehot_used, 2 * UT)
            pe.sem_inc(xs_turned, 2)
            pe.sem_inc(down_done, 2)
            pe.wait_ge(proj_in, 16 * len(FIRST_LOADS))
            pipeline(pe, step_1)

            def sums_of_squares(u, par):
                pe.wait_ge(sq_ready, u + 1)
                if isinstance(u, int) and u == 0:
                    pe.wait_ge(logits_ready, UNITS + 2)
                for j in range(UT):
                    ins = pe.matmul(squares_ps[:, bass.ds(H * (UT * u + j), H)], k_sq[:, par, P * j:P * j + P],
                                    heads[:], start=True, stop=True)
                ins.then_inc(ss_done, 1)

            def keys_product(u, par):
                wait(pe, k_ready, u - 1)
                unit_product(bank[2 + par], K, u).then_inc(k_done, 1)

            pe.wait_ge(logits_t_ready, UNITS)
            pe.wait_ge(consts_in, 16 * len(EARLY_LOADS))
            def early_keys(units):
                for u in units:
                    keys_product(u, u % 2)
                    if u > 0:
                        sums_of_squares(u - 1, 1 - u % 2)

            early_keys(range(KEYS_FIRST // 2))

            pe.wait_ge(pool_consts, POOL_CONSTS)
            pe.wait_ge(chosen_ready, 1)
            chosen_flat = chosen[:].rearrange("p e t -> p (e t)")
            pe.matmul(bank[0], below[:], chosen_flat, start=True, stop=True)
            pe.matmul(bank[1], ones_b[:], chosen_flat, start=True, stop=True).then_inc(counts_done, 1)
            early_keys(range(KEYS_FIRST // 2, KEYS_FIRST))
            pe.wait_ge(folded, 2)
            table_ps = bank[7][:, 0:TABLE]
            pe.matmul(table_ps, zero_r[:, 0:P], zero_r[:], start=True, stop=False)

            STEPS = UNITS // 2
            KEYS = (UNITS - KEYS_FIRST) // 2
            with pe.Fori(0, 2) as i:
                done = 0
                for step in range(2 * STEPS):
                    u = STEPS * i + step // 2
                    for m in range(UT * (step % 2), UT * (step % 2) + UT):
                        pe.wait_ge(onehot_ready, 2 * UT * u + m + 1)
                        if m in POOL_ROWS:
                            pe.wait_ge(pool_row_ready, len(POOL_ROWS) * (u + 2) + POOL_ROWS.index(m) + 1)
                        pe.matmul(table_ps, is_row[:, m], is_tile[:, m], start=False, stop=False
                                  ).then_inc(onehot_used, 1)
                    if (step + 2) * KEYS // STEPS > done < 2 * KEYS:
                        key, par = KEYS_FIRST + KEYS * i + done // 2, done // 2 % 2
                        if done % 2 == 0:
                            keys_product(key, par)
                        else:
                            sums_of_squares(key - 1, 1 - par)
                        done += 1
            pe.matmul(table_ps, zero_r[:, 0:P], zero_r[:], start=False, stop=True).then_inc(table_done, 1)
            sums_of_squares(UNITS - 1, 1)

            pe.wait_ge(routed, 1)
            pe.wait_ge(ss_ready, 2)

            def turn_slots(b, h):
                pe.wait_ge(rows_in[h], 32 * b + 32)
                for s in range(SUBS):
                    ins = pe.transpose(bank[6 + h][:, P * s:P * s + P], slot_rows[:, h, s], ident[:])
                ins.then_inc(xs_turned, 1)

            def up(b, h, ep):
                pe.wait_ge(xs_ready, 2 * b + h + 1)
                for c in range(HC):
                    n = (2 * b + h) * HC + c
                    pe.wait_ge(hidden_ready, n + 1)
                    for which, out_ps in ((1, g_ps[c]), (0, h_ps[c])):
                        cols = slice(P * c, P * c + P)
                        ins = product3(out_ps, w_hi[:, ep, which, cols], w_lo[:, ep, which, cols],
                                       xs_hi[:, h], xs_lo[:, h])
                    ins.then_inc(up_done, 1)

            def down(b, h, ep):
                n = 2 * b + h
                pe.wait_ge(hidden_ready, HC * n + 2 * HC)
                pe.wait_ge(y_ready, n + 1)
                for s in range(SUBS):
                    for c in range(HC):
                        ins = pe.matmul(bank[4 + h][:, D * s:D * s + D], hidden[:, h, c, P * s:P * s + P],
                                        w2_s[:, ep, c], start=(c == 0), stop=(c == HC - 1))
                ins.then_inc(down_done, 1)

            for h in range(2):
                turn_slots(0, h)
            with pe.Fori(0, E // 2) as pair:
                for ep in range(2):
                    e = 2 * pair + ep
                    start, end = block_range(pe, e)
                    pe.wait_ge(w_split, e + 1)
                    pe.wait_ge(w2_in[ep], 16 * pair + 16)
                    stand_apart(pe)
                    with pe.Fori(start, end) as b:
                        up(b, 0, ep)
                        up(b, 1, ep)
                        turn_slots(b + 1, 0)
                        down(b, 0, ep)
                        turn_slots(b + 1, 1)
                        down(b, 1, ep)

            total = all_blocks(pe)

            def project(u, i):
                wait(pe, proj_read, 4 * u + i)
                unit_product(proj_ps, (V, F, Q, G)[i], u).then_inc(proj_done, 1)

            def turn_norms(u, par):
                pe.wait_ge(inv_ready_u, u + 1)
                wait(pe, bn_o_ready, u - 1)
                for j in range(UT):
                    rows = inv_u[:, par, H * j:H * j + H].rearrange("p h k -> p (h k)")
                    ins = pe.transpose(turn_ps[:, P * j:P * j + P], rows, ident[:])
                ins.then_inc(inv_turned, 1)

            def spread_v(u, par, v):
                at = HD * u + v
                if v == 0:
                    pe.wait_ge(v_lo_ready, u + 1)
                if v >= 3:
                    pe.wait_ge(kv_ready, at - 2)
                elif v < 2:
                    wait(pe, kv_ready, at - 1)
                pe.matmul(spread_ps[v], spread[:, v], v_hi[:, par], start=True, stop=False)
                pe.matmul(spread_ps[v], spread[:, v], v_lo[:, par], start=False, stop=True
                          ).then_inc(spread_done, 1)

            def collect_v(u, par, v):
                if v in POOL_V:
                    pe.wait_ge(qs_pool, len(POOL_V) * u + POOL_V.index(v) + 1)
                else:
                    pe.wait_ge(qs_dve, len(DVE_V) * u + DVE_V.index(v) + 1)
                if v == 0:
                    wait(pe, o_ready, u - 1)
                pe.matmul(o_ps[par], collect[:, v], q_state[:, v], start=(v == 0), stop=(v == HD - 1)
                          ).then_inc(collected, 1)

            def turn_outputs(u, par):
                pe.wait_ge(o_ready, u + 1)
                wait(pe, kn_ready, u + 1)
                for j in range(UT):
                    ins = pe.transpose(turn_ps[:, D * j:D * j + D], o_s[:, par, P * j:P * j + P], ident[:])
                ins.then_inc(o_turned, 1)

            def output_product(u, par):
                wait(pe, attn_ready, u)
                for j in range(UT):
                    ins = pe.matmul(wo_ps[:, D * j:D * j + D], o_s[:, par, P * j:P * j + P], wo_c[:],
                                    start=True, stop=True)
                ins.then_inc(out_done, 1)

            def step(u, par, k, first, last):
                for v in range(HD):
                    if v + 3 < HD:
                        spread_v(u, par, v + 3)
                    elif not last:
                        spread_v(u + 1, 1 - par, v + 3 - HD)
                    if v > 0:
                        collect_v(u, par, v - 1)
                    elif not first:
                        collect_v(u - 1, 1 - par, HD - 1)
                    if v == 2 and not first:
                        turn_outputs(u - 1, 1 - par)
                    if v == 3 and not first:
                        output_product(u - 1, 1 - par)
                    if not last:
                        if v < 2:
                            project(u + 1, v)
                        if v == 4:
                            turn_norms(u + 1, 1 - par)
                        if v == 5 or v == 6:
                            project(u + 1, v - 3)

            for i in range(4):
                project(0, i)
            pe.wait_ge(y_ready, 2 * total + 2)
            turn_norms(0, 0)
            for v in range(3):
                spread_v(0, 0, v)
            pe.wait_ge(experts_over, 1)
            units_in_steps(pe, step)
            collect_v(UNITS - 1, 1, HD - 1)
            turn_outputs(UNITS - 1, 1)
            output_product(UNITS - 1, 1)


def kernel(L0_attn_x, L0_attn_Wq, L0_attn_Wk, L0_attn_Wv, L0_attn_Wf, L0_attn_Wg1, L0_attn_Wg2, L0_attn_ln_w,
           L0_attn_Wo, L0_ffn_Wg, L0_ffn_bg, L0_ffn_W0, L0_ffn_b0, L0_ffn_W1, L0_ffn_b1, L0_ffn_W2, L0_ffn_b2):
    import concourse.bacc as bacc
    from concourse.bass_utils import run_bass_kernel_spmd

    f32 = np.float32
    a = {k: np.asarray(v) for k, v in dict(
        x=L0_attn_x, Wq=L0_attn_Wq, Wk=L0_attn_Wk, Wv=L0_attn_Wv, Wf=L0_attn_Wf, Wg1=L0_attn_Wg1, Wg2=L0_attn_Wg2,
        ln_w=L0_attn_ln_w, Wo=L0_attn_Wo, Wg=L0_ffn_Wg, bg=L0_ffn_bg, W0=L0_ffn_W0, b0=L0_ffn_b0, W1=L0_ffn_W1,
        b1=L0_ffn_b1, W2=L0_ffn_W2, b2=L0_ffn_b2).items()}
    w_proj = np.zeros((D, 5, D), f32)
    w_proj[:, 0] = a["Wq"].T
    w_proj[:, 1] = a["Wk"].T
    w_proj[:, 2] = a["Wv"].T
    w_proj[:, 3] = np.repeat(a["Wf"].T, HD, axis=1)
    w_proj[:, 4, :E] = a["Wg"]
    row, col = np.arange(P)[:, None], np.arange(P)[None, :]
    spread = np.stack([(row == (col // HD) * HD + v) for v in range(HD)], axis=1).astype(f32)
    collect = np.stack([(row // HD == col // HD) & (col % HD == v) for v in range(HD)], axis=1).astype(f32) * f32(0.5)
    token = row + P * np.arange(TILES)[None, :] - T // 2
    arrays = dict(
        x=a["x"].reshape(T, D),
        w_proj=w_proj,
        wg1=a["Wg1"],
        wg2t=a["Wg2"].T,
        wot=a["Wo"].T,
        ln_w=a["ln_w"].reshape(D, 1),
        gate_b=np.broadcast_to(a["bg"].reshape(1, 1, E), (P, UT, E)),
        w0=a["W0"],
        w1=a["W1"],
        w2=a["W2"].reshape(E, HC, P, D).transpose(0, 2, 1, 3),
        b0=a["b0"].reshape(E * HC, P).T,
        b1=a["b1"].reshape(E * HC, P).T,
        b2=np.broadcast_to(a["b2"].reshape(1, E * D), (P, E * D)),
        ident_in=np.eye(P, dtype=f32),
        below_in=(row < col).astype(f32),
        heads_in=(row // HD == np.arange(H)[None, :]).astype(f32),
        spread_in=spread,
        collect_in=collect,
        center_in=np.eye(P, dtype=f32) - f32(1.0 / P),
        iota_in=np.broadcast_to(np.arange(TABLE)[None, :], (P, TABLE)).astype(f32),
        token_in=token.astype(f32),
        rank_in=np.broadcast_to((E - np.arange(E)).reshape(1, E, 1), (P, E, TILES)).astype(f32),
    )
    nc = bacc.Bacc("TRN2", target_bir_lowering=False, num_devices=1)
    args, given = {}, {}
    for name, array in arrays.items():
        given[f"in_{name}"] = np.ascontiguousarray(array)
        args[name] = nc.dram_tensor(f"in_{name}", array.shape, mybir.dt.from_np(array.dtype),
                                    kind="ExternalInput").ap()
    args["out"] = nc.dram_tensor("out_rows", (T, D), F32, kind="ExternalOutput").ap()
    build(nc, **args)
    got = run_bass_kernel_spmd(nc, [given], core_ids=[0]).results[0]["out_rows"]
    return got.reshape(T // SEQ, SEQ, D)
```
